# Optimizing a Trainium2 kernel written in Bass

```python
import numpy as np
import jax
import jax.numpy as jnp

def _softmax(x, axis=-1):
    return jax.nn.softmax(x, axis=axis)

def _gelu(x):
    return jax.nn.gelu(x, approximate=True)

def _silu(x):
    return jax.nn.silu(x)

def _sigmoid(x):
    return jax.nn.sigmoid(x)

def _layernorm(x, axis=-1, eps=1e-05):
    m = jnp.mean(x, axis=axis, keepdims=True)
    v = jnp.var(x, axis=axis, keepdims=True)
    return (x - m) / jnp.sqrt(v + eps)

def _scatter_add(tgt, idx, src, axis=0):
    return tgt.at[idx].add(src)

def _segment_sum(src, seg, n):
    return jax.ops.segment_sum(src, seg, n)
kernel_name = 'mk_xattn_seq_d1_seqx_r4_473709'

def setup_inputs(seed: int=0):
    np.random.seed(seed)
    _w = jnp.asarray

    def _rec_inputs():
        import jax
        import jax.numpy as jnp
        _rk = jax.random.key(seed)
        x = -0.000125 + 0.9999 * jax.random.normal(jax.random.fold_in(_rk, 1), (2, 512, 512), jnp.float32)
        _lenS = 512 - jax.random.randint(jax.random.fold_in(_rk, 7), (2,), 0, max(1, 512 // 4) + 1, jnp.int32)
        _lenS2 = 1024 - jax.random.randint(jax.random.fold_in(_rk, 8), (2,), 0, max(1, 1024 // 4) + 1, jnp.int32)
        _ctx_1024P = jax.random.normal(jax.random.fold_in(_rk, 11), (2, 16, 256), jnp.float32)
        _ctx_1024c = jax.random.dirichlet(jax.random.fold_in(_rk, 511), 0.3 * jnp.ones((16,), jnp.float32), (2, 1024))
        _ctx_1024t = jnp.einsum('bsk,bkd->bsd', _ctx_1024c, _ctx_1024P)
        _ctx_1024t = _ctx_1024t * jax.lax.rsqrt(jnp.mean(jnp.square(_ctx_1024t)) + 1e-12) * 0.953939
        ctx_1024 = 4.13588e-05 + 0.999923 * (_ctx_1024t + 0.3 * jax.random.normal(jax.random.fold_in(_rk, 611), (2, 1024, 256), jnp.float32))
        return (x, ctx_1024)
    x, ctx_1024 = _rec_inputs()

    def _L0_xattn_setup():
        import jax, jax.numpy as jnp
        import numpy as np
        EPS = 1e-06

        def _rmsnorm(x, w):
            var = jnp.mean(jnp.square(x), axis=-1, keepdims=True)
            return x * jax.lax.rsqrt(var + EPS) * w
        key = jax.random.key(seed)
        ks = jax.random.split(key, 6)
        B, N, M = (4, 1024, 512)
        d_model, memory_dim = (512, 256)
        hidden_states = jax.random.normal(ks[0], (B, N, d_model), dtype=jnp.float32)
        memory = jax.random.normal(ks[1], (B, M, memory_dim), dtype=jnp.float32)
        W_mem = jax.random.normal(ks[2], (d_model, memory_dim), dtype=jnp.float32) / np.sqrt(memory_dim)
        W_gate = jax.random.normal(ks[3], (d_model, 2 * d_model), dtype=jnp.float32) / np.sqrt(2 * d_model)
        b_gate = jax.random.normal(ks[4], (d_model,), dtype=jnp.float32) * 0.01
        norm_w = jnp.ones((d_model,), dtype=jnp.float32)
        return {'hidden_states': hidden_states, 'memory': memory, 'W_mem': W_mem, 'W_gate': W_gate, 'b_gate': b_gate, 'norm_w': norm_w}
    _L0_xattn_all = _L0_xattn_setup()
    _L0_xattn_in = {k: v for k, v in _L0_xattn_all.items() if k in ('W_mem', 'W_gate', 'b_gate', 'norm_w')}
    del _L0_xattn_all
    return {'x': x, 'ctx_1024': ctx_1024, 'L0_xattn_W_mem': _L0_xattn_in['W_mem'], 'L0_xattn_W_gate': _L0_xattn_in['W_gate'], 'L0_xattn_b_gate': _L0_xattn_in['b_gate'], 'L0_xattn_norm_w': _L0_xattn_in['norm_w']}

def reference(x, ctx_1024, L0_xattn_W_mem, L0_xattn_W_gate, L0_xattn_b_gate, L0_xattn_norm_w):
    import jax
    import jax.numpy as jnp

    def _L0_xattn_ref(hidden_states, memory, W_mem, W_gate, b_gate, norm_w):
        import jax, jax.numpy as jnp
        import numpy as np
        EPS = 1e-06

        def _rmsnorm(x, w):
            var = jnp.mean(jnp.square(x), axis=-1, keepdims=True)
            return x * jax.lax.rsqrt(var + EPS) * w
        D = hidden_states.shape[-1]
        memory_proj = jnp.einsum('bme,de->bmd', memory, W_mem)
        scores = jnp.einsum('bnd,bmd->bnm', hidden_states, memory_proj) / jnp.sqrt(jnp.float32(D))
        attn = jax.nn.softmax(scores, axis=-1)
        memory_context = jnp.einsum('bnm,bmd->bnd', attn, memory_proj)
        gate_input = jnp.concatenate([hidden_states, memory_context], axis=-1)
        gate = jax.nn.sigmoid(jnp.einsum('bnf,df->bnd', gate_input, W_gate) + b_gate)
        fused = hidden_states + gate * memory_context
        return _rmsnorm(fused, norm_w)
    x = _L0_xattn_ref(x, ctx_1024, L0_xattn_W_mem, L0_xattn_W_gate, L0_xattn_b_gate, L0_xattn_norm_w)
    return x

_drawn_inputs = setup_inputs


def setup_inputs(seed=0):
    import zlib

    import numpy as np

    out = dict(_drawn_inputs(seed))
    spreads = {'L0_xattn_norm_w': (1.0, 0.2)}
    factors = {'L0_xattn_b_gate': 53.777}
    for name, (base, spread) in spreads.items():
        noise = np.random.default_rng([zlib.crc32(name.encode()), seed]).standard_normal(out[name].shape)
        drawn = base * np.exp(spread * noise) if base else spread * noise
        out[name] = jnp.asarray(drawn.astype(out[name].dtype))
    for name, factor in factors.items():
        out[name] = (out[name] * factor).astype(out[name].dtype)
    return out
```

```python
import concourse.bass as bass
from concourse import mybir
from contextlib import ExitStack


def xattn_kernel(nc, xT, ctxT, ctxN, w_mem, w_memT, w_gateT, x_rows, b_gate, norm_w, out):
    f32 = mybir.dt.float32
    f32r = mybir.dt.float32r
    ALU = mybir.AluOpType
    ACT = mybir.ActivationFunctionType
    AX = mybir.AxisListType

    P = 128
    B, _, KD, N = xT.shape
    KE, M = ctxT.shape[2:]
    KM = M // P
    D, E = KD * P, KE * P
    T = N // P
    BANK = 512
    SCALE = float(D) ** -0.5
    EPS = 1e-6
    RING = 8
    WARM = 8
    assert N == BANK and D == BANK and M == 2 * BANK and KE == 2 and T == 4

    ctx = ExitStack()
    with ctx:
        def sb(name, shape, dt=f32):
            return ctx.enter_context(nc.sbuf_tensor(name, shape, dt))

        def pair(name, shape):
            return sb(name + "_hi", shape, f32r), sb(name + "_lo", shape, f32r)

        def sem(name):
            return ctx.enter_context(nc.semaphore(name))

        xT_s = pair("xT", [P, B, KD, N])
        ctxT_s = pair("ctxT", [P, KE, M])
        ctxN_s = pair("ctxN", [P, KM, E])
        wm_s = pair("wm", [P, KE, KD, P])
        wmT_s = pair("wmT", [P, KE, D])
        wgT_s = pair("wgT", [P, 2 * KD, D])
        qT_s = pair("qT", [P, KE, N])
        aT_s = pair("aT", [P, KE, N])
        pT_s = pair("pT", [P, KM, N])
        wcT_s = [w[:].rearrange("p c k n -> p c (k n)") for w in wm_s]

        ring = sb("ring", [P, RING, BANK])
        probs = sb("probs", [P, 2, M])
        ident = sb("ident", [P, P])
        warm = sb("warm", [P, BANK], mybir.dt.bfloat16)
        one = sb("one", [P, 1])
        bias = sb("bias", [P, D])
        gain = sb("gain", [P, D])
        xr = sb("xr", [P, 2, D])
        gx = sb("gx", [P, 2, D])
        gate = sb("gate", [P, 2, D])
        res = sb("res", [P, 2, D])
        neg_max = sb("neg_max", [P, B * T])
        row_sum = sb("row_sum", [P, B * T])
        inv_sum = sb("inv_sum", [P, B * T])
        half_inv = sb("half_inv", [P, B * T])
        ssq = sb("ssq", [P, B * T])
        mean_sq = sb("mean_sq", [P, B * T])
        rstd = sb("rstd", [P, B * T])
        neg_half = sb("neg_half", [P, 1])

        wide = ctx.enter_context(nc.psum_tensor("wide", [P, 4, BANK], f32))
        acc = ctx.enter_context(nc.psum_tensor("acc", [P, 2, BANK], f32))
        turn = ctx.enter_context(nc.psum_tensor("turn", [P, 2, BANK], f32))

        blocks = []

        def block(src, dst, kind):
            blocks.append((src, dst[0], dst[1], kind))

        def part(operand, *index):
            return [o[(slice(None), *index)] for o in operand]

        def wm_block(c):
            block(w_mem[:, c], part(wm_s, c), "wm")

        def xT_block(b, k):
            block(xT[b, :, k], part(xT_s, b, k), "xT")

        def ctxT_block(b, c, h):
            cols = slice(h * BANK, (h + 1) * BANK)
            block(ctxT[b, :, c, cols], part(ctxT_s, c, cols), f"ctxT{b}")

        def ctxN_block(b, j):
            rows = slice(2 * j, 2 * j + 2)
            block(ctxN[b, :, rows], part(ctxN_s, rows), f"ctxN{b}")

        def wgT_block(k):
            block(w_gateT[:, k], part(wgT_s, k), "wgT")

        wm_block(0)
        for k in range(KD):
            xT_block(0, k)
        wm_block(1)
        for c in range(KE):
            for h in range(2):
                ctxT_block(0, c, h)
        for k in range(KD):
            xT_block(1, k)
        for k in range(KD, 2 * KD):
            wgT_block(k)
        for j in range(KM // 2):
            ctxN_block(0, j)
        for c in range(KE):
            for h in range(2):
                ctxT_block(1, c, h)
        for k in range(KD):
            wgT_block(k)
        for c in range(KE):
            block(w_memT[:, c], part(wmT_s, c), "wmT")
        for j in range(KM // 2):
            ctxN_block(1, j)
        NB = len(blocks)
        WM0, XT0, WM1, CT0, XT1, WG2, CN0, CT1, WG1, WMT, CN1 = 0, 1, 5, 6, 10, 14, 18, 22, 26, 30, 32

        ON_DVE = set(range(0, 8)) | {10, 12, 23, 25}
        dve_lo = [i for i in range(NB) if i in ON_DVE]
        pool_lo = [i for i in range(NB) if i not in ON_DVE]

        loaded = [sem(f"loaded{i}") for i in range(NB)]
        vec_loaded = sem("vec_loaded")
        x_loaded = [sem(f"x_loaded{i}") for i in range(2)]
        stored = [sem(f"stored{i}") for i in range(2)]
        warm_set = sem("warm_set")
        ident_set = sem("ident_set")
        one_set = sem("one_set")
        neg_half_set = sem("neg_half_set")
        act_ready = sem("act_ready")
        hi_done = sem("hi_done")
        lo_dve = sem("lo_dve")
        lo_pool = sem("lo_pool")
        q_sum = sem("q_sum")
        scores_sum = sem("scores_sum")
        turned = sem("turned")
        wc_sum = sem("wc_sum")
        a_sum = sem("a_sum")
        gx_sum = sem("gx_sum")
        ga_sum = sem("ga_sum")
        mc_sum = sem("mc_sum")
        q_hi, q_lo = sem("q_hi"), sem("q_lo")
        max_done = sem("max_done")
        probs_done = sem("probs_done")
        pT_hi, pT_lo = sem("pT_hi"), sem("pT_lo")
        wc_hi, wc_lo = sem("wc_hi"), sem("wc_lo")
        a_hi, a_lo = sem("a_hi"), sem("a_lo")
        inv_done = sem("inv_done")
        half_done = sem("half_done")
        gx_done = sem("gx_done")
        arg_done = sem("arg_done")
        tanh_done = sem("tanh_done")
        gated = sem("gated")
        fused = sem("fused")
        squared = sem("squared")
        mean_done = sem("mean_done")
        rstd_done = sem("rstd_done")
        res_done = sem("res_done")

        def nth_tile(b, t):
            return T * b + t + 1

        def nth_turn(b, t, h):
            return 2 * (T * b + t) + h + 1

        def nth_chunk(b, c):
            return KE * b + c + 1

        def bank_of(b, t, use):
            return (3 * (T * b + t) + use) % 4

        def wait_lo(eng, i):
            if i in ON_DVE:
                eng.wait_ge(lo_dve, dve_lo.index(i) + 1)
            else:
                eng.wait_ge(lo_pool, pool_lo.index(i) + 1)

        def wait_place(eng, kind):
            if kind == "ctxT1":
                eng.wait_ge(scores_sum, nth_tile(0, T - 1))
            if kind == "ctxN1":
                eng.wait_ge(a_sum, nth_chunk(0, KE - 1))

        block_ctx = ctx.enter_context(nc.Block())

        @block_ctx.sync
        def _(sp):
            def load_x(j):
                sp.dma_start(xr[:, j % 2], x_rows[j]).then_inc(x_loaded[j % 2], 16)

            for i, (src, _, _, _) in enumerate(blocks):
                if i >= RING:
                    sp.wait_ge(hi_done, i - RING + 1)
                    wait_lo(sp, i - RING)
                dst = ring[:, i % RING]
                if len(src.shape) == 3:
                    dst = dst.rearrange("p (a c) -> p a c", a=src.shape[1])
                sp.dma_start(dst, src).then_inc(loaded[i], 16)
                if i == CT0:
                    sp.dma_start(bias[:], b_gate.partition_broadcast(P)).then_inc(vec_loaded, 16)
                    sp.dma_start(gain[:], norm_w.partition_broadcast(P)).then_inc(vec_loaded, 16)
                if i == WG1:
                    load_x(0)
                    load_x(1)
            for j in range(B * T):
                sp.wait_ge(res_done, j + 1)
                sp.dma_start(out[j], res[:, j % 2]).then_inc(stored[j % 2], 16)
                if j + 2 < B * T:
                    load_x(j + 2)
            for done in stored:
                sp.wait_ge(done, 16 * B * T // 2)

        @block_ctx.gpsimd
        def _(pool):
            nc.gpsimd.memset(ident[:], 0.0).then_inc(ident_set, 1)
            nc.gpsimd.memset(neg_half[:], -0.5).then_inc(neg_half_set, 1)
            pool.wait_ge(ident_set, 1)
            nc.gpsimd.affine_select(out=ident[:], in_=ident[:], compare_op=ALU.not_equal, fill=1.0,
                                    base=0, pattern=[[-1, P]], channel_multiplier=1).then_inc(ident_set, 1)
            pool.wait_ge(neg_half_set, 1)

            def split_lo(i):
                _, hi, lo, kind = blocks[i]
                pool.wait_ge(hi_done, i + 1)
                wait_place(pool, kind)
                src = ring[:, i % RING]
                if len(hi.shape) == 3:
                    src = src.rearrange("p (a c) -> p a c", a=hi.shape[1])
                nc.gpsimd.tensor_tensor(lo, src, hi.bitcast(f32), ALU.subtract).then_inc(lo_pool, 1)

            def norm_factor(j):
                pool.wait_ge(squared, j + 1)
                col = slice(j, j + 1)
                nc.gpsimd.tensor_scalar(mean_sq[:, col], ssq[:, col], 1.0 / D, EPS,
                                        ALU.mult, ALU.add).then_inc(mean_done, 1)
                pool.wait_ge(mean_done, j + 1)
                nc.gpsimd.tensor_tensor(rstd[:, col], mean_sq[:, col], neg_half[:], ALU.pow)\
                    .then_inc(rstd_done, 1)

            for i in pool_lo:
                split_lo(i)
            for j in range(B * T):
                norm_factor(j)

        @block_ctx.scalar
        def _(act):
            act.wait_ge(one_set, 1)
            nc.scalar.activation(one[:], one[:], ACT.Exp).then_inc(act_ready, 1)

            def split_hi(*ids):
                for i in ids:
                    _, hi, _, kind = blocks[i]
                    act.wait_ge(loaded[i], 16)
                    wait_place(act, kind)
                    src = ring[:, i % RING]
                    if len(hi.shape) == 3:
                        src = src.rearrange("p (a c) -> p a c", a=hi.shape[1])
                    nc.scalar.activation(hi, src, ACT.Copy).then_inc(hi_done, 1)

            def query_hi(b, c):
                act.wait_ge(q_sum, nth_chunk(b, c))
                if b:
                    act.wait_ge(scores_sum, nth_tile(b - 1, T - 1))
                nc.scalar.activation(qT_s[0][:, c], acc[:, c], ACT.Copy, scale=SCALE).then_inc(q_hi, 1)

            def softmax(b, t):
                j = T * b + t
                act.wait_ge(max_done, nth_tile(b, t))
                if j >= 2:
                    act.wait_ge(turned, 2 * (j - 1))
                nc.scalar.activation(probs[:, j % 2], wide[:, 2 * (t % 2):2 * (t % 2) + 2], ACT.Exp,
                                     bias=neg_max[:, j:j + 1], accum_out=row_sum[:, j:j + 1])\
                    .then_inc(probs_done, 1)

            def turned_hi(b, t):
                for h in range(2):
                    act.wait_ge(turned, nth_turn(b, t, h))
                    if b and t == 0 and h == 0:
                        act.wait_ge(a_sum, nth_chunk(b - 1, KE - 1))
                    nc.scalar.activation(pT_s[0][:, 4 * h:4 * h + 4, t * P:(t + 1) * P],
                                         turn[:, h].rearrange("p (k n) -> p k n", k=4), ACT.Copy)\
                        .then_inc(pT_hi, 1)

            def weight_hi(c):
                act.wait_ge(wc_sum, c + 1)
                nc.scalar.activation(wcT_s[0][:, c], wide[:, c], ACT.Copy).then_inc(wc_hi, 1)

            def attended_hi(b, c):
                act.wait_ge(a_sum, nth_chunk(b, c))
                if b:
                    act.wait_ge(mc_sum, nth_tile(b - 1, T - 1))
                nc.scalar.activation(aT_s[0][:, c], acc[:, c], ACT.Copy).then_inc(a_hi, 1)

            def gate_tanh(j):
                act.wait_ge(arg_done, j + 1)
                nc.scalar.activation(gate[:, j % 2], gate[:, j % 2], ACT.Tanh, scale=0.5)\
                    .then_inc(tanh_done, 1)

            def squares(j):
                act.wait_ge(fused, j + 1)
                if j >= 2:
                    act.wait_ge(stored[j % 2], 16 * (j // 2))
                nc.scalar.activation(res[:, j % 2], gate[:, j % 2], ACT.Square,
                                     accum_out=ssq[:, j:j + 1]).then_inc(squared, 1)

            split_hi(0, 1, 2, 3, 4, 5, 6, 7)
            query_hi(0, 0)
            split_hi(8, 9)
            query_hi(0, 1)
            split_hi(10, 11)
            softmax(0, 0)
            split_hi(12, 13)
            softmax(0, 1)
            split_hi(14, 15)
            softmax(0, 2)
            turned_hi(0, 0)
            split_hi(16)
            softmax(0, 3)
            turned_hi(0, 1)
            query_hi(1, 0)
            split_hi(17, 18)
            turned_hi(0, 2)
            split_hi(19, 20)
            query_hi(1, 1)
            turned_hi(0, 3)
            split_hi(21, 22, 23, 24)
            weight_hi(0)
            split_hi(25, 26)
            weight_hi(1)
            split_hi(27, 28, 29, 30, 31)
            attended_hi(0, 0)
            attended_hi(0, 1)
            split_hi(32, 33)
            softmax(1, 0)
            split_hi(34, 35)
            softmax(1, 1)
            softmax(1, 2)
            turned_hi(1, 0)
            softmax(1, 3)
            turned_hi(1, 1)
            turned_hi(1, 2)
            gate_tanh(0)
            squares(0)
            turned_hi(1, 3)
            gate_tanh(1)
            squares(1)
            for j in range(2, T):
                gate_tanh(j)
                squares(j)
            attended_hi(1, 0)
            attended_hi(1, 1)
            for j in range(T, B * T):
                gate_tanh(j)
                squares(j)

        @block_ctx.vector
        def _(dve):
            nc.vector.memset(warm[:], 0.0).then_inc(warm_set, 1)
            nc.vector.memset(one[:], 1.0).then_inc(one_set, 1)

            def split_lo(*ids):
                for i in ids:
                    _, hi, lo, kind = blocks[i]
                    dve.wait_ge(hi_done, i + 1)
                    wait_place(dve, kind)
                    src = ring[:, i % RING]
                    if len(hi.shape) == 3:
                        src = src.rearrange("p (a c) -> p a c", a=hi.shape[1])
                    nc.vector.tensor_tensor(lo, src, hi.bitcast(f32), ALU.subtract).then_inc(lo_dve, 1)

            def query_lo(b, c):
                dve.wait_ge(q_hi, nth_chunk(b, c))
                nc.vector.scalar_tensor_tensor(out=qT_s[1][:, c], in0=acc[:, c], scalar=SCALE,
                                               in1=qT_s[0][:, c].bitcast(f32), op0=ALU.mult,
                                               op1=ALU.subtract).then_inc(q_lo, 1)

            def row_max(b, t):
                j = T * b + t
                dve.wait_ge(scores_sum, nth_tile(b, t))
                nc.vector.tensor_reduce(neg_max[:, j:j + 1], wide[:, 2 * (t % 2):2 * (t % 2) + 2],
                                        AX.XY, ALU.max, negate=True).then_inc(max_done, 1)

            def turned_lo(b, t):
                for h in range(2):
                    dve.wait_ge(pT_hi, nth_turn(b, t, h))
                    place = (slice(None), slice(4 * h, 4 * h + 4), slice(t * P, (t + 1) * P))
                    nc.vector.tensor_tensor(pT_s[1][place], turn[:, h].rearrange("p (k n) -> p k n", k=4),
                                            pT_s[0][place].bitcast(f32), ALU.subtract).then_inc(pT_lo, 1)

            def weight_lo(c):
                dve.wait_ge(wc_hi, c + 1)
                nc.vector.tensor_tensor(wcT_s[1][:, c], wide[:, c], wcT_s[0][:, c].bitcast(f32),
                                        ALU.subtract).then_inc(wc_lo, 1)

            def attended_lo(b, c):
                dve.wait_ge(a_hi, nth_chunk(b, c))
                nc.vector.tensor_tensor(aT_s[1][:, c], acc[:, c], aT_s[0][:, c].bitcast(f32),
                                        ALU.subtract).then_inc(a_lo, 1)

            def inverses(b):
                cols = slice(T * b, T * b + T)
                dve.wait_ge(probs_done, T * (b + 1))
                nc.vector.reciprocal(inv_sum[:, cols], row_sum[:, cols]).then_inc(inv_done, 1)
                dve.wait_ge(inv_done, b + 1)
                nc.vector.tensor_scalar(half_inv[:, cols], inv_sum[:, cols], 0.5, None, ALU.mult)\
                    .then_inc(half_done, 1)

            def gate_x(b, t):
                j = T * b + t
                if j == 0:
                    dve.wait_ge(vec_loaded, 32)
                dve.wait_ge(gx_sum, j + 1)
                nc.vector.tensor_tensor(gx[:, j % 2], wide[:, bank_of(b, t, 0)], bias[:], ALU.add)\
                    .then_inc(gx_done, 1)

            def gate_arg(b, t):
                j = T * b + t
                dve.wait_ge(gx_done, j + 1)
                dve.wait_ge(ga_sum, j + 1)
                if j >= 2:
                    dve.wait_ge(res_done, j - 1)
                nc.vector.scalar_tensor_tensor(out=gate[:, j % 2], in0=wide[:, bank_of(b, t, 1)],
                                               scalar=inv_sum[:, j:j + 1], in1=gx[:, j % 2],
                                               op0=ALU.mult, op1=ALU.add).then_inc(arg_done, 1)

            def gated_context(b, t):
                j = T * b + t
                dve.wait_ge(tanh_done, j + 1)
                dve.wait_ge(mc_sum, j + 1)
                nc.vector.scalar_tensor_tensor(out=gate[:, j % 2], in0=gate[:, j % 2], scalar=1.0,
                                               in1=wide[:, bank_of(b, t, 2)], op0=ALU.add,
                                               op1=ALU.mult).then_inc(gated, 1)

            def fuse(b, t):
                j = T * b + t
                dve.wait_ge(gated, j + 1)
                dve.wait_ge(x_loaded[j % 2], 16 * (j // 2 + 1))
                nc.vector.scalar_tensor_tensor(out=gate[:, j % 2], in0=gate[:, j % 2],
                                               scalar=half_inv[:, j:j + 1], in1=xr[:, j % 2],
                                               op0=ALU.mult, op1=ALU.add).then_inc(fused, 1)

            def normalize(j):
                dve.wait_ge(rstd_done, j + 1)
                nc.vector.scalar_tensor_tensor(out=res[:, j % 2], in0=gate[:, j % 2],
                                               scalar=rstd[:, j:j + 1], in1=gain[:],
                                               op0=ALU.mult, op1=ALU.mult).then_inc(res_done, 1)

            split_lo(0, 1, 2, 3, 4, 5, 6, 7)
            query_lo(0, 0)
            query_lo(0, 1)
            split_lo(10)
            row_max(0, 0)
            split_lo(12)
            row_max(0, 1)
            row_max(0, 2)
            turned_lo(0, 0)
            row_max(0, 3)
            turned_lo(0, 1)
            query_lo(1, 0)
            turned_lo(0, 2)
            query_lo(1, 1)
            turned_lo(0, 3)
            inverses(0)
            split_lo(23)
            weight_lo(0)
            weight_lo(1)
            split_lo(25)
            attended_lo(0, 0)
            attended_lo(0, 1)
            row_max(1, 0)
            row_max(1, 1)
            row_max(1, 2)
            turned_lo(1, 0)
            row_max(1, 3)
            turned_lo(1, 1)
            inverses(1)
            gate_x(0, 0)
            turned_lo(1, 2)
            gate_arg(0, 0)
            gated_context(0, 0)
            fuse(0, 0)
            gate_x(0, 1)
            turned_lo(1, 3)
            normalize(0)
            gate_arg(0, 1)
            gated_context(0, 1)
            fuse(0, 1)
            for t in range(2, T):
                gate_x(0, t)
                normalize(t - 1)
                gate_arg(0, t)
                gated_context(0, t)
                fuse(0, t)
            normalize(T - 1)
            attended_lo(1, 0)
            attended_lo(1, 1)
            for t in range(T):
                gate_x(1, t)
                if t:
                    normalize(T + t - 1)
                gate_arg(1, t)
                gated_context(1, t)
                fuse(1, t)
            normalize(2 * T - 1)

        @block_ctx.tensor
        def _(pe):
            HI, LO = 0, 1
            PASSES = ((HI, HI), (HI, LO), (LO, HI))

            def product(psum, terms, done):
                n = 0
                for left, right in PASSES:
                    for stationary, moving, wait in terms:
                        if (left, right) == (HI, HI) and wait is not None:
                            wait(HI)
                        if (left, right) == (HI, LO) and wait is not None:
                            wait(LO)
                        last = nc.tensor.matmul(psum, stationary(left), moving(right), start=(n == 0),
                                                stop=(n == 3 * len(terms) - 1))
                        n += 1
                last.then_inc(done, 1)

            def input_wait(*ids):
                def wait(half):
                    for i in ids:
                        if half == HI:
                            pe.wait_ge(hi_done, i + 1)
                        else:
                            wait_lo(pe, i)
                return wait

            def queries(b, c):
                if b:
                    pe.wait_ge(q_lo, nth_chunk(b - 1, c))
                product(acc[:, c],
                        [(lambda s, k=k: wm_s[s][:, c, k], lambda s, k=k: xT_s[s][:, b, k],
                          input_wait((WM0, WM1)[c], (XT0, XT1)[b] + k)) for k in range(KD)], q_sum)

            def scores(b, t):
                if t >= 2:
                    pe.wait_ge(probs_done, nth_tile(b, t - 2))
                elif b:
                    pe.wait_ge(wc_lo, KE)
                rows = slice(t * P, (t + 1) * P)
                for h in range(2):
                    cols = slice(h * BANK, (h + 1) * BANK)
                    n = 0
                    for left, right in PASSES:
                        for c in range(KE):
                            if t == 0:
                                if h == 0:
                                    if (left, right) == (HI, HI):
                                        pe.wait_ge(q_hi, nth_chunk(b, c))
                                    if (left, right) == (LO, HI):
                                        pe.wait_ge(q_lo, nth_chunk(b, c))
                                if (left, right) == (HI, HI):
                                    pe.wait_ge(hi_done, (CT0, CT1)[b] + 2 * c + h + 1)
                                if (left, right) == (HI, LO):
                                    wait_lo(pe, (CT0, CT1)[b] + 2 * c + h)
                            last = nc.tensor.matmul(wide[:, 2 * (t % 2) + h], qT_s[left][:, c, rows],
                                                    ctxT_s[right][:, c, cols], start=(n == 0),
                                                    stop=(n == 3 * KE - 1))
                            n += 1
                last.then_inc(scores_sum, 1)

            def transposes(b, t):
                j = T * b + t
                if j == 0:
                    pe.wait_ge(ident_set, 2)
                pe.wait_ge(probs_done, j + 1)
                for h in range(2):
                    if j:
                        pe.wait_ge(pT_lo, 2 * (j - 1) + h + 1)
                    for k in range(4):
                        m = (4 * h + k) * P
                        last = nc.tensor.transpose(turn[:, h, k * P:(k + 1) * P],
                                                   probs[:, j % 2, m:m + P], ident[:])
                    last.then_inc(turned, 1)

            def gate_weights(c):
                pe.wait_ge(probs_done, nth_tile(0, 2))
                product(wide[:, c],
                        [(lambda s, k=k: wm_s[s][:, c, k], lambda s, k=k: wgT_s[s][:, KD + k],
                          input_wait(WG2 + k)) for k in range(KD)], wc_sum)

            def attended(b, c):
                if b == 0:
                    pe.wait_ge(q_lo, nth_chunk(1, c))
                else:
                    pe.wait_ge(a_lo, nth_chunk(b - 1, c))
                if c == 0:
                    pe.wait_ge(pT_lo, nth_turn(b, T - 1, 1))
                cols = slice(c * P, (c + 1) * P)
                product(acc[:, c],
                        [(lambda s, k=k: ctxN_s[s][:, k, cols], lambda s, k=k: pT_s[s][:, k],
                          input_wait((CN0, CN1)[b] + k // 2) if c == 0 else None)
                         for k in range(KM)], a_sum)

            def bank_free(b, t, use):
                n = 3 * (T * b + t) + use - 4
                if n < 0:
                    pe.wait_ge(probs_done, B * T - 1 + (n + 4) // 2)
                else:
                    pe.wait_ge((gx_done, arg_done, gated)[n % 3], n // 3 + 1)

            def gate_from_x(b, t):
                bank_free(b, t, 0)
                rows = slice(t * P, (t + 1) * P)
                product(wide[:, bank_of(b, t, 0)],
                        [(lambda s, k=k: xT_s[s][:, b, k, rows], lambda s, k=k: wgT_s[s][:, k],
                          input_wait(WG1 + k) if b == t == 0 else None) for k in range(KD)], gx_sum)

            def from_attended(b, t):
                rows = slice(t * P, (t + 1) * P)
                if t == 0:
                    pe.wait_ge(a_lo, nth_chunk(b, KE - 1))
                if b == t == 0:
                    pe.wait_ge(wc_lo, KE)
                bank_free(b, t, 1)
                product(wide[:, bank_of(b, t, 1)],
                        [(lambda s, c=c: aT_s[s][:, c, rows], lambda s, c=c: wcT_s[s][:, c], None)
                         for c in range(KE)], ga_sum)
                bank_free(b, t, 2)
                product(wide[:, bank_of(b, t, 2)],
                        [(lambda s, c=c: aT_s[s][:, c, rows], lambda s, c=c: wmT_s[s][:, c],
                          input_wait(WMT + c) if b == t == 0 else None) for c in range(KE)], mc_sum)

            pe.wait_ge(warm_set, 1)
            for _ in range(WARM):
                nc.tensor.matmul(turn[:, 0], warm[:, 0:P], warm[:], start=True, stop=True)
            queries(0, 0)
            queries(0, 1)
            scores(0, 0)
            scores(0, 1)
            scores(0, 2)
            transposes(0, 0)
            scores(0, 3)
            transposes(0, 1)
            queries(1, 0)
            transposes(0, 2)
            queries(1, 1)
            transposes(0, 3)
            gate_weights(0)
            gate_weights(1)
            attended(0, 0)
            attended(0, 1)
            scores(1, 0)
            scores(1, 1)
            scores(1, 2)
            transposes(1, 0)
            scores(1, 3)
            transposes(1, 1)
            gate_from_x(0, 0)
            transposes(1, 2)
            from_attended(0, 0)
            gate_from_x(0, 1)
            transposes(1, 3)
            from_attended(0, 1)
            for t in range(2, T):
                gate_from_x(0, t)
                from_attended(0, t)
            attended(1, 0)
            attended(1, 1)
            for t in range(T):
                gate_from_x(1, t)
                from_attended(1, t)


def kernel(x, ctx_1024, L0_xattn_W_mem, L0_xattn_W_gate, L0_xattn_b_gate, L0_xattn_norm_w):
    import numpy as np
    import concourse.bacc as bacc
    from concourse.bass_utils import run_bass_kernel_spmd

    P = 128
    x, mem, wm, wg = (np.asarray(a) for a in (x, ctx_1024, L0_xattn_W_mem, L0_xattn_W_gate))
    B, N, D = x.shape
    M, E = mem.shape[1:]
    KD, KE, KM = D // P, E // P, M // P
    arrays = {
        "xT": x.reshape(B, N, KD, P).transpose(0, 3, 2, 1),
        "ctxT": mem.reshape(B, M, KE, P).transpose(0, 3, 2, 1),
        "ctxN": mem.reshape(B, KM, P, E).transpose(0, 2, 1, 3),
        "w_mem": wm.reshape(KD, P, KE, P).transpose(1, 2, 0, 3),
        "w_memT": wm.reshape(D, KE, P).transpose(2, 1, 0),
        "w_gateT": wg.reshape(D, 2 * KD, P).transpose(2, 1, 0),
        "x_rows": x.reshape(B * N // P, P, D),
        "b_gate": np.asarray(L0_xattn_b_gate),
        "norm_w": np.asarray(L0_xattn_norm_w),
    }
    arrays = {name: np.ascontiguousarray(a) for name, a in arrays.items()}
    nc = bacc.Bacc("TRN2", target_bir_lowering=False, num_devices=1)
    args = [nc.dram_tensor(name, a.shape, mybir.dt.from_np(a.dtype), kind="ExternalInput").ap()
            for name, a in arrays.items()]
    out = nc.dram_tensor("out", (B * N // P, P, D), mybir.dt.float32, kind="ExternalOutput").ap()
    xattn_kernel(nc, *args, out)
    r = run_bass_kernel_spmd(nc, [arrays], core_ids=[0])
    return r.results[0]["out"].reshape(B, N, D)
```

```python
import concourse.bass as bass
from concourse import mybir
from contextlib import ExitStack


def xattn_kernel(nc, xT, ctxT, ctxN, w_mem, w_memT, w_gateT, x_rows, b_gate, norm_w, out):
    f32 = mybir.dt.float32
    f32r = mybir.dt.float32r
    ALU = mybir.AluOpType
    ACT = mybir.ActivationFunctionType
    AX = mybir.AxisListType

    P = 128
    B, _, KD, N = xT.shape
    KE, M = ctxT.shape[2:]
    KM = M // P
    D, E = KD * P, KE * P
    T = N // P
    BANK = 512
    SCALE = float(D) ** -0.5
    EPS = 1e-6
    RING = 8
    WARM = 35
    assert N == BANK and D == BANK and M == 2 * BANK and KE == 2 and T == 4

    ctx = ExitStack()
    with ctx:
        def sb(name, shape, dt=f32):
            return ctx.enter_context(nc.sbuf_tensor(name, shape, dt))

        def pair(name, shape):
            return sb(name + "_hi", shape, f32r), sb(name + "_lo", shape, f32r)

        def sem(name):
            return ctx.enter_context(nc.semaphore(name))

        xT_s = pair("xT", [P, B, KD, N])
        ctxT_s = pair("ctxT", [P, KE, M])
        ctxN_s = pair("ctxN", [P, KM, E])
        wm_s = pair("wm", [P, KE, KD, P])
        wmT_s = pair("wmT", [P, KE, D])
        wgT_s = pair("wgT", [P, 2 * KD, D])
        qT_s = pair("qT", [P, KE, N])
        aT_s = pair("aT", [P, KE, N])
        pT_s = pair("pT", [P, KM, N])
        wcT_s = [w[:].rearrange("p c k n -> p c (k n)") for w in wm_s]

        ring = sb("ring", [P, RING, BANK])
        probs = sb("probs", [P, 2, M])
        ident = sb("ident", [P, P])
        warm = sb("warm", [P, P], mybir.dt.bfloat16)
        one = sb("one", [P, 1])
        bias = sb("bias", [P, D])
        gain = sb("gain", [P, D])
        xr = sb("xr", [P, 2, D])
        gx = sb("gx", [P, 2, D])
        gate = sb("gate", [P, 2, D])
        res = sb("res", [P, 2, D])
        neg_max = sb("neg_max", [P, B * T])
        row_sum = sb("row_sum", [P, B * T])
        inv_sum = sb("inv_sum", [P, B * T])
        half_inv = sb("half_inv", [P, B * T])
        mean_sq = sb("mean_sq", [P, B * T + 1])
        rstd = sb("rstd", [P, B * T])
        neg_half = sb("neg_half", [P, 1])

        wide = ctx.enter_context(nc.psum_tensor("wide", [P, 4, BANK], f32))
        acc = ctx.enter_context(nc.psum_tensor("acc", [P, 2, BANK], f32))
        turn = ctx.enter_context(nc.psum_tensor("turn", [P, 2, BANK], f32))

        blocks = []
        index_of = {}

        def block(key, src, operand, *place):
            hi, lo = (o[(slice(None), *place)] for o in operand)
            index_of[key] = len(blocks)
            blocks.append((src, hi, lo, key))

        def wm_block(c, half):
            ks = slice(half * KD // 2, (half + 1) * KD // 2)
            block(("wm", c, half), w_mem[:, c, ks], wm_s, c, ks)

        def xT_block(b, k):
            block(("xT", b, k), xT[b, :, k], xT_s, b, k)

        def ctxT_block(b, c, h):
            cols = slice(h * BANK, (h + 1) * BANK)
            block(("ctxT", b, c, h), ctxT[b, :, c, cols], ctxT_s, c, cols)

        def ctxN_block(b, j):
            rows = slice(2 * j, 2 * j + 2)
            block(("ctxN", b, j), ctxN[b, :, rows], ctxN_s, rows)

        def wgT_block(k):
            block(("wgT", k), w_gateT[:, k], wgT_s, k)

        wm_block(0, 0)
        xT_block(0, 0)
        xT_block(0, 1)
        wm_block(1, 0)
        wm_block(0, 1)
        xT_block(0, 2)
        xT_block(0, 3)
        wm_block(1, 1)
        for c in range(KE):
            for h in range(2):
                ctxT_block(0, c, h)
        for k in range(KD):
            xT_block(1, k)
        for k in range(KD, 2 * KD):
            wgT_block(k)
        for j in range(KM // 2):
            ctxN_block(0, j)
        for c in range(KE):
            for h in range(2):
                ctxT_block(1, c, h)
        for k in range(KD):
            wgT_block(k)
        for c in range(KE):
            block(("wmT", c), w_memT[:, c], wmT_s, c)
        for j in range(KM // 2):
            ctxN_block(1, j)
        NB = len(blocks)
        LAST = B * T - 1
        HALVES = (slice(0, D // 2), slice(D // 2, D))

        def slot(i):
            hi = blocks[i][1]
            if len(hi.shape) == 2:
                return ring[:, i % RING, 0:hi.shape[1]]
            a, c = hi.shape[1:]
            return ring[:, i % RING, 0:a * c].rearrange("p (a c) -> p a c", a=a)

        ON_DVE = set(range(0, 12)) | {25, 27}
        dve_lo = [i for i in range(NB) if i in ON_DVE]
        pool_lo = [i for i in range(NB) if i not in ON_DVE]

        loaded = [sem(f"loaded{i}") for i in range(NB)]
        vec_loaded = sem("vec_loaded")
        x_loaded = [sem(f"x_loaded{i}") for i in range(2)]
        stored = [sem(f"stored{i}") for i in range(2)]
        warm_set = sem("warm_set")
        ident_set = sem("ident_set")
        one_set = sem("one_set")
        neg_half_set = sem("neg_half_set")
        act_ready = sem("act_ready")
        hi_done = sem("hi_done")
        lo_dve = sem("lo_dve")
        lo_pool = sem("lo_pool")
        q_sum = sem("q_sum")
        scores_sum = sem("scores_sum")
        turned = sem("turned")
        wc_sum = sem("wc_sum")
        a_sum = sem("a_sum")
        gx_sum = sem("gx_sum")
        ga_sum = sem("ga_sum")
        mc_sum = sem("mc_sum")
        q_hi, q_lo = sem("q_hi"), sem("q_lo")
        max_done = sem("max_done")
        probs_done = sem("probs_done")
        pT_hi, pT_lo = sem("pT_hi"), sem("pT_lo")
        wc_hi, wc_lo = sem("wc_hi"), sem("wc_lo")
        a_hi, a_lo = sem("a_hi"), sem("a_lo")
        inv_done = sem("inv_done")
        half_done = sem("half_done")
        gx_done = sem("gx_done")
        arg_done = sem("arg_done")
        tanh_done = sem("tanh_done")
        gated = sem("gated")
        fused = sem("fused")
        mc_half = sem("mc_half")
        gated_half, fused_half = sem("gated_half"), sem("fused_half")
        gained, last_gained = sem("gained"), sem("last_gained")
        mean_done = sem("mean_done")
        rstd_done = sem("rstd_done")
        res_done = sem("res_done")
        last_res = sem("last_res")

        def nth_tile(b, t):
            return T * b + t + 1

        def nth_turn(b, t, h):
            return 2 * (T * b + t) + h + 1

        def nth_chunk(b, c):
            return KE * b + c + 1

        def bank_of(b, t, use):
            return (3 * (T * b + t) + use) % 4

        last_banks = (bank_of(B - 1, T - 1, 2), bank_of(B, 0, 0))

        def wait_lo(eng, i):
            if i in ON_DVE:
                eng.wait_ge(lo_dve, dve_lo.index(i) + 1)
            else:
                eng.wait_ge(lo_pool, pool_lo.index(i) + 1)

        def wait_place(eng, key):
            if key[0:2] == ("ctxT", 1):
                eng.wait_ge(scores_sum, nth_tile(0, T - 1))
            if key[0:2] == ("ctxN", 1):
                eng.wait_ge(a_sum, nth_chunk(0, KE - 1))

        block_ctx = ctx.enter_context(nc.Block())

        @block_ctx.sync
        def _(sp):
            def load_x(j):
                sp.dma_start(xr[:, j % 2], x_rows[j]).then_inc(x_loaded[j % 2], 16)

            for i, (src, _, _, key) in enumerate(blocks):
                if i >= RING:
                    sp.wait_ge(hi_done, i - RING + 1)
                    wait_lo(sp, i - RING)
                sp.dma_start(slot(i), src).then_inc(loaded[i], 16)
                if key == ("xT", 1, KD - 1):
                    sp.dma_start(bias[:], b_gate.partition_broadcast(P)).then_inc(vec_loaded, 16)
                    sp.dma_start(gain[:], norm_w.partition_broadcast(P)).then_inc(vec_loaded, 16)
                if key == ("wgT", 0):
                    load_x(0)
                    load_x(1)
            for j in range(LAST):
                sp.wait_ge(res_done, j + 1)
                sp.dma_start(out[j], res[:, j % 2]).then_inc(stored[j % 2], 16)
                if j + 2 < B * T:
                    load_x(j + 2)
            sp.wait_ge(last_res, 1)
            sp.dma_start(out[LAST], res[:, LAST % 2]).then_inc(stored[LAST % 2], 16)
            for done in stored:
                sp.wait_ge(done, 16 * B * T // 2)

        @block_ctx.gpsimd
        def _(pool):
            nc.gpsimd.memset(ident[:], 0.0).then_inc(ident_set, 1)
            nc.gpsimd.memset(neg_half[:], -0.5).then_inc(neg_half_set, 1)
            pool.wait_ge(ident_set, 1)
            nc.gpsimd.affine_select(out=ident[:], in_=ident[:], compare_op=ALU.not_equal, fill=1.0,
                                    base=0, pattern=[[-1, P]], channel_multiplier=1).then_inc(ident_set, 1)

            def split_lo(i):
                _, hi, lo, key = blocks[i]
                pool.wait_ge(hi_done, i + 1)
                wait_place(pool, key)
                nc.gpsimd.tensor_tensor(lo, slot(i), hi.bitcast(f32), ALU.subtract).then_inc(lo_pool, 1)

            def gain_rows(j):
                pool.wait_ge(fused, j + 1)
                if j == 0:
                    pool.wait_ge(vec_loaded, 32)
                if j >= 2:
                    pool.wait_ge(stored[j % 2], 16 * (j // 2))
                nc.gpsimd.tensor_tensor(res[:, j % 2], gate[:, j % 2], gain[:], ALU.mult)\
                    .then_inc(gained, 1)

            def norm_factor(j):
                pool.wait_ge(mean_done, j + 1 + (j == LAST))
                col = slice(j, j + 1)
                nc.gpsimd.tensor_tensor(rstd[:, col], mean_sq[:, j + (j == LAST):j + (j == LAST) + 1],
                                        neg_half[:], ALU.pow).then_inc(rstd_done, 1)

            for i in pool_lo:
                split_lo(i)
            pool.wait_ge(neg_half_set, 1)
            for j in range(LAST):
                gain_rows(j)
                norm_factor(j)
            norm_factor(LAST)

        @block_ctx.scalar
        def _(act):
            act.wait_ge(one_set, 1)
            nc.scalar.activation(one[:], one[:], ACT.Exp).then_inc(act_ready, 1)

            def split_hi(*ids):
                for i in ids:
                    _, hi, _, key = blocks[i]
                    act.wait_ge(loaded[i], 16)
                    wait_place(act, key)
                    nc.scalar.activation(hi, slot(i), ACT.Copy).then_inc(hi_done, 1)

            def query_hi(b, c):
                act.wait_ge(q_sum, nth_chunk(b, c))
                if b:
                    act.wait_ge(scores_sum, nth_tile(b - 1, T - 1))
                nc.scalar.activation(qT_s[0][:, c], acc[:, c], ACT.Copy, scale=SCALE).then_inc(q_hi, 1)

            def softmax(b, t):
                j = T * b + t
                act.wait_ge(max_done, nth_tile(b, t))
                if j >= 2:
                    act.wait_ge(turned, 2 * (j - 1))
                nc.scalar.activation(probs[:, j % 2], wide[:, 2 * (t % 2):2 * (t % 2) + 2], ACT.Exp,
                                     bias=neg_max[:, j:j + 1], accum_out=row_sum[:, j:j + 1])\
                    .then_inc(probs_done, 1)

            def turned_hi(b, t):
                for h in range(2):
                    act.wait_ge(turned, nth_turn(b, t, h))
                    if b and t == 0 and h == 0:
                        act.wait_ge(a_sum, nth_chunk(b - 1, KE - 1))
                    nc.scalar.activation(pT_s[0][:, 4 * h:4 * h + 4, t * P:(t + 1) * P],
                                         turn[:, h].rearrange("p (k n) -> p k n", k=4), ACT.Copy)\
                        .then_inc(pT_hi, 1)

            def weight_hi(c):
                act.wait_ge(wc_sum, c + 1)
                nc.scalar.activation(wcT_s[0][:, c], wide[:, c], ACT.Copy).then_inc(wc_hi, 1)

            def attended_hi(b, c):
                act.wait_ge(a_sum, nth_chunk(b, c))
                if b:
                    act.wait_ge(mc_sum, nth_tile(b - 1, T - 1))
                nc.scalar.activation(aT_s[0][:, c], acc[:, c], ACT.Copy).then_inc(a_hi, 1)

            def gate_tanh(j):
                act.wait_ge(arg_done, j + 1)
                nc.scalar.activation(gate[:, j % 2], gate[:, j % 2], ACT.Tanh, scale=0.5)\
                    .then_inc(tanh_done, 1)

            def normalize(j):
                act.wait_ge(gained, j + 1)
                act.wait_ge(rstd_done, j + 1)
                nc.scalar.activation(res[:, j % 2], res[:, j % 2], ACT.Copy,
                                     scale=rstd[:, j:j + 1]).then_inc(res_done, 1)

            split_hi(0, 1, 2, 3, 4, 5, 6, 7, 8, 9)
            query_hi(0, 0)
            split_hi(10, 11)
            query_hi(0, 1)
            split_hi(12, 13, 14)
            softmax(0, 0)
            split_hi(15, 16)
            softmax(0, 1)
            split_hi(17)
            turned_hi(0, 0)
            softmax(0, 2)
            split_hi(18, 19)
            turned_hi(0, 1)
            softmax(0, 3)
            split_hi(20)
            query_hi(1, 0)
            turned_hi(0, 2)
            split_hi(21, 22)
            query_hi(1, 1)
            turned_hi(0, 3)
            split_hi(23, 24, 25, 26)
            weight_hi(0)
            split_hi(27, 28)
            weight_hi(1)
            split_hi(29, 30, 31, 32, 33)
            attended_hi(0, 0)
            attended_hi(0, 1)
            split_hi(34, 35)
            softmax(1, 0)
            split_hi(36, 37)
            softmax(1, 1)
            turned_hi(1, 0)
            softmax(1, 2)
            turned_hi(1, 1)
            softmax(1, 3)
            turned_hi(1, 2)
            gate_tanh(0)
            turned_hi(1, 3)
            normalize(0)
            for j in range(1, T):
                gate_tanh(j)
                normalize(j)
            attended_hi(1, 0)
            attended_hi(1, 1)
            for j in range(T, LAST):
                gate_tanh(j)
                normalize(j)
            for h, cols in enumerate(HALVES):
                act.wait_ge(arg_done, LAST + h + 1)
                nc.scalar.activation(gate[:, LAST % 2, cols], gate[:, LAST % 2, cols], ACT.Tanh, scale=0.5)\
                    .then_inc(tanh_done, 1)

        @block_ctx.vector
        def _(dve):
            nc.vector.memset(warm[:].bitcast(mybir.dt.uint32), 0).then_inc(warm_set, 1)
            nc.vector.memset(one[:], 1.0).then_inc(one_set, 1)

            def split_lo(*ids):
                for i in ids:
                    _, hi, lo, key = blocks[i]
                    dve.wait_ge(hi_done, i + 1)
                    wait_place(dve, key)
                    nc.vector.tensor_tensor(lo, slot(i), hi.bitcast(f32), ALU.subtract).then_inc(lo_dve, 1)

            def query_lo(b, c):
                dve.wait_ge(q_hi, nth_chunk(b, c))
                nc.vector.scalar_tensor_tensor(out=qT_s[1][:, c], in0=acc[:, c], scalar=SCALE,
                                               in1=qT_s[0][:, c].bitcast(f32), op0=ALU.mult,
                                               op1=ALU.subtract).then_inc(q_lo, 1)

            def row_max(b, t):
                j = T * b + t
                dve.wait_ge(scores_sum, nth_tile(b, t))
                nc.vector.tensor_reduce(neg_max[:, j:j + 1], wide[:, 2 * (t % 2):2 * (t % 2) + 2],
                                        AX.XY, ALU.max, negate=True).then_inc(max_done, 1)

            def turned_lo(b, t):
                for h in range(2):
                    dve.wait_ge(pT_hi, nth_turn(b, t, h))
                    place = (slice(None), slice(4 * h, 4 * h + 4), slice(t * P, (t + 1) * P))
                    nc.vector.tensor_tensor(pT_s[1][place], turn[:, h].rearrange("p (k n) -> p k n", k=4),
                                            pT_s[0][place].bitcast(f32), ALU.subtract).then_inc(pT_lo, 1)

            def weight_lo(c):
                dve.wait_ge(wc_hi, c + 1)
                nc.vector.tensor_tensor(wcT_s[1][:, c], wide[:, c], wcT_s[0][:, c].bitcast(f32),
                                        ALU.subtract).then_inc(wc_lo, 1)

            def attended_lo(b, c):
                dve.wait_ge(a_hi, nth_chunk(b, c))
                nc.vector.tensor_tensor(aT_s[1][:, c], acc[:, c], aT_s[0][:, c].bitcast(f32),
                                        ALU.subtract).then_inc(a_lo, 1)

            def inverses(b):
                cols = slice(T * b, T * b + T)
                dve.wait_ge(probs_done, T * (b + 1))
                nc.vector.reciprocal(inv_sum[:, cols], row_sum[:, cols]).then_inc(inv_done, 1)
                dve.wait_ge(inv_done, b + 1)
                nc.vector.tensor_scalar(half_inv[:, cols], inv_sum[:, cols], 0.5, None, ALU.mult)\
                    .then_inc(half_done, 1)

            def gate_x(b, t):
                j = T * b + t
                if j == 0:
                    dve.wait_ge(vec_loaded, 32)
                dve.wait_ge(gx_sum, j + 1)
                nc.vector.tensor_tensor(gx[:, j % 2], wide[:, bank_of(b, t, 0)], bias[:], ALU.add)\
                    .then_inc(gx_done, 1)

            def gate_arg(b, t):
                j = T * b + t
                dve.wait_ge(gx_done, j + 1)
                dve.wait_ge(ga_sum, j + 1)
                if j >= 2:
                    dve.wait_ge(gained, j - 1)
                    dve.wait_ge(mean_done, j - 1)
                nc.vector.scalar_tensor_tensor(out=gate[:, j % 2], in0=wide[:, bank_of(b, t, 1)],
                                               scalar=inv_sum[:, j:j + 1], in1=gx[:, j % 2],
                                               op0=ALU.mult, op1=ALU.add).then_inc(arg_done, 1)

            def gated_context(b, t):
                j = T * b + t
                dve.wait_ge(tanh_done, j + 1)
                dve.wait_ge(mc_sum, j + 1)
                nc.vector.scalar_tensor_tensor(out=gate[:, j % 2], in0=gate[:, j % 2], scalar=1.0,
                                               in1=wide[:, bank_of(b, t, 2)], op0=ALU.add,
                                               op1=ALU.mult).then_inc(gated, 1)

            def fuse(b, t):
                j = T * b + t
                dve.wait_ge(gated, j + 1)
                dve.wait_ge(x_loaded[j % 2], 16 * (j // 2 + 1))
                nc.vector.scalar_tensor_tensor(out=gate[:, j % 2], in0=gate[:, j % 2],
                                               scalar=half_inv[:, j:j + 1], in1=xr[:, j % 2],
                                               op0=ALU.mult, op1=ALU.add).then_inc(fused, 1)

            def mean_square(j):
                dve.wait_ge(fused, j + 1)
                nc.vector.tensor_tensor_reduce(gx[:, j % 2], gate[:, j % 2], gate[:, j % 2], 1.0 / D, EPS,
                                               ALU.mult, ALU.add, mean_sq[:, j:j + 1]).then_inc(mean_done, 1)

            def finish(b, t):
                gated_context(b, t)
                fuse(b, t)
                mean_square(T * b + t)

            def finish_last():
                n = LAST % 2
                dve.wait_ge(gx_done, LAST + 1)
                dve.wait_ge(ga_sum, LAST + 1)
                dve.wait_ge(gained, LAST - 1)
                for cols in HALVES:
                    nc.vector.scalar_tensor_tensor(out=gate[:, n, cols],
                                                   in0=wide[:, bank_of(B - 1, T - 1, 1), cols],
                                                   scalar=inv_sum[:, LAST:], in1=gx[:, n, cols],
                                                   op0=ALU.mult, op1=ALU.add).then_inc(arg_done, 1)
                for h, cols in enumerate(HALVES):
                    dve.wait_ge(tanh_done, LAST + h + 1)
                    dve.wait_ge(mc_half, h + 1)
                    nc.vector.scalar_tensor_tensor(out=gate[:, n, cols], in0=gate[:, n, cols],
                                                   scalar=1.0, in1=wide[:, last_banks[h], cols],
                                                   op0=ALU.add, op1=ALU.mult).then_inc(gated_half, 1)
                dve.wait_ge(x_loaded[n], 16 * (LAST // 2 + 1))
                for h, cols in enumerate(HALVES):
                    dve.wait_ge(gated_half, h + 1)
                    nc.vector.scalar_tensor_tensor(out=gate[:, n, cols], in0=gate[:, n, cols],
                                                   scalar=half_inv[:, LAST:], in1=xr[:, n, cols],
                                                   op0=ALU.mult, op1=ALU.add).then_inc(fused_half, 1)
                start = EPS
                for h, cols in enumerate(HALVES):
                    dve.wait_ge(fused_half, h + 1)
                    nc.vector.tensor_tensor_reduce(gx[:, n, cols], gate[:, n, cols], gate[:, n, cols],
                                                   1.0 / D, start, ALU.mult, ALU.add,
                                                   mean_sq[:, LAST + h:LAST + h + 1]).then_inc(mean_done, 1)
                    dve.wait_ge(mean_done, LAST + 1)
                    start = mean_sq[:, LAST:LAST + 1]
                dve.wait_ge(stored[n], 16 * (LAST // 2))
                nc.vector.tensor_tensor(res[:, n], gate[:, n], gain[:], ALU.mult).then_inc(last_gained, 1)
                dve.wait_ge(last_gained, 1)
                dve.wait_ge(rstd_done, LAST + 1)
                nc.vector.tensor_scalar(res[:, n], res[:, n], rstd[:, LAST:], None, ALU.mult)\
                    .then_inc(last_res, 1)

            split_lo(0, 1, 2, 3, 4, 5, 6, 7, 8, 9)
            query_lo(0, 0)
            split_lo(10, 11)
            query_lo(0, 1)
            row_max(0, 0)
            row_max(0, 1)
            row_max(0, 2)
            turned_lo(0, 0)
            row_max(0, 3)
            turned_lo(0, 1)
            query_lo(1, 0)
            turned_lo(0, 2)
            query_lo(1, 1)
            turned_lo(0, 3)
            inverses(0)
            split_lo(25)
            weight_lo(0)
            weight_lo(1)
            split_lo(27)
            attended_lo(0, 0)
            attended_lo(0, 1)
            row_max(1, 0)
            row_max(1, 1)
            row_max(1, 2)
            turned_lo(1, 0)
            row_max(1, 3)
            turned_lo(1, 1)
            inverses(1)
            gate_x(0, 0)
            turned_lo(1, 2)
            gate_arg(0, 0)
            finish(0, 0)
            gate_x(0, 1)
            turned_lo(1, 3)
            gate_arg(0, 1)
            finish(0, 1)
            for t in range(2, T):
                gate_x(0, t)
                gate_arg(0, t)
                finish(0, t)
            attended_lo(1, 0)
            attended_lo(1, 1)
            for t in range(T - 1):
                gate_x(1, t)
                gate_arg(1, t)
                finish(1, t)
            gate_x(1, T - 1)
            finish_last()

        @block_ctx.tensor
        def _(pe):
            HI, LO = 0, 1
            PASSES = ((HI, HI), (HI, LO), (LO, HI))

            def keep_warm(n):
                for _ in range(n):
                    nc.tensor.matmul(turn[:, 0, 0:P], warm[:], warm[:], start=True, stop=True)

            def product(psum, terms, done):
                n = 0
                for left, right in PASSES:
                    for stationary, moving, wait in terms:
                        if (left, right) == (HI, HI) and wait is not None:
                            wait(HI)
                        if (left, right) == (HI, LO) and wait is not None:
                            wait(LO)
                        last = nc.tensor.matmul(psum, stationary(left), moving(right), start=(n == 0),
                                                stop=(n == 3 * len(terms) - 1))
                        n += 1
                last.then_inc(done, 1)

            def input_wait(key):
                def wait(half):
                    if half == HI:
                        pe.wait_ge(hi_done, index_of[key] + 1)
                    else:
                        wait_lo(pe, index_of[key])
                return wait

            def queries(b, c, ks):
                if b and ks[0] == 0:
                    pe.wait_ge(q_lo, nth_chunk(b - 1, c))
                for k in ks:
                    wm_i, xT_i = index_of["wm", c, 2 * k // KD], index_of["xT", b, k]
                    for left, right in ((HI, HI), (LO, HI), (HI, LO)):
                        if (left, right) == (HI, HI):
                            pe.wait_ge(hi_done, max(wm_i, xT_i) + 1)
                        elif left == LO:
                            wait_lo(pe, wm_i)
                        else:
                            wait_lo(pe, xT_i)
                        last = nc.tensor.matmul(acc[:, c], wm_s[left][:, c, k], xT_s[right][:, b, k],
                                                start=(k == 0 and (left, right) == (HI, HI)),
                                                stop=(k == KD - 1 and (left, right) == (HI, LO)))
                if ks[-1] == KD - 1:
                    last.then_inc(q_sum, 1)

            def scores(b, t):
                if t >= 2:
                    pe.wait_ge(probs_done, nth_tile(b, t - 2))
                elif b:
                    pe.wait_ge(wc_lo, KE)
                rows = slice(t * P, (t + 1) * P)
                for c in range(KE):
                    for left, right in PASSES:
                        if t == 0 and (left, right) == (HI, HI):
                            pe.wait_ge(q_hi, nth_chunk(b, c))
                        if t == 0 and left == LO:
                            pe.wait_ge(q_lo, nth_chunk(b, c))
                        for h in range(2):
                            i = index_of["ctxT", b, c, h]
                            if t == 0 and (left, right) == (HI, HI):
                                pe.wait_ge(hi_done, i + 1)
                            if t == 0 and right == LO:
                                wait_lo(pe, i)
                            last = nc.tensor.matmul(wide[:, 2 * (t % 2) + h], qT_s[left][:, c, rows],
                                                    ctxT_s[right][:, c, h * BANK:(h + 1) * BANK],
                                                    start=(c == 0 and (left, right) == (HI, HI)),
                                                    stop=(c == KE - 1 and left == LO))
                last.then_inc(scores_sum, 1)

            def transposes(b, t):
                j = T * b + t
                if j == 0:
                    pe.wait_ge(ident_set, 2)
                pe.wait_ge(probs_done, j + 1)
                for h in range(2):
                    if j:
                        pe.wait_ge(pT_lo, 2 * (j - 1) + h + 1)
                    for k in range(4):
                        m = (4 * h + k) * P
                        last = nc.tensor.transpose(turn[:, h, k * P:(k + 1) * P],
                                                   probs[:, j % 2, m:m + P], ident[:])
                    last.then_inc(turned, 1)

            def gate_weights(c):
                pe.wait_ge(probs_done, nth_tile(0, 2))
                product(wide[:, c],
                        [(lambda s, k=k: wm_s[s][:, c, k], lambda s, k=k: wgT_s[s][:, KD + k],
                          input_wait(("wgT", KD + k))) for k in range(KD)], wc_sum)

            def attended(b, c):
                if b == 0:
                    pe.wait_ge(q_lo, nth_chunk(1, c))
                else:
                    pe.wait_ge(a_lo, nth_chunk(b - 1, c))
                if c == 0:
                    pe.wait_ge(pT_lo, nth_turn(b, T - 1, 1))
                cols = slice(c * P, (c + 1) * P)
                product(acc[:, c],
                        [(lambda s, k=k: ctxN_s[s][:, k, cols], lambda s, k=k: pT_s[s][:, k],
                          input_wait(("ctxN", b, k // 2)) if c == 0 else None)
                         for k in range(KM)], a_sum)

            def bank_free(b, t, use):
                n = 3 * (T * b + t) + use - 4
                if n < 0:
                    pe.wait_ge(probs_done, B * T - 1 + (n + 4) // 2)
                else:
                    pe.wait_ge((gx_done, arg_done, gated)[n % 3], n // 3 + 1)

            def gate_from_x(b, t):
                bank_free(b, t, 0)
                rows = slice(t * P, (t + 1) * P)
                product(wide[:, bank_of(b, t, 0)],
                        [(lambda s, k=k: xT_s[s][:, b, k, rows], lambda s, k=k: wgT_s[s][:, k],
                          input_wait(("wgT", k)) if b == t == 0 else None) for k in range(KD)], gx_sum)

            def from_attended(b, t):
                rows = slice(t * P, (t + 1) * P)
                if t == 0:
                    pe.wait_ge(a_lo, nth_chunk(b, KE - 1))
                if b == t == 0:
                    pe.wait_ge(wc_lo, KE)
                bank_free(b, t, 1)
                product(wide[:, bank_of(b, t, 1)],
                        [(lambda s, c=c: aT_s[s][:, c, rows], lambda s, c=c: wcT_s[s][:, c], None)
                         for c in range(KE)], ga_sum)
                bank_free(b, t, 2)
                if T * b + t == LAST:
                    pe.wait_ge(gated, LAST)
                    for h, cols in enumerate(HALVES):
                        product(wide[:, last_banks[h], cols],
                                [(lambda s, c=c: aT_s[s][:, c, rows], lambda s, c=c: wmT_s[s][:, c, cols],
                                  None) for c in range(KE)], mc_half)
                    return
                product(wide[:, bank_of(b, t, 2)],
                        [(lambda s, c=c: aT_s[s][:, c, rows], lambda s, c=c: wmT_s[s][:, c],
                          input_wait(("wmT", c)) if b == t == 0 else None) for c in range(KE)], mc_sum)

            pe.wait_ge(warm_set, 1)
            keep_warm(WARM)
            halves = (range(0, KD // 2), range(KD // 2, KD))
            for ks in halves:
                for c in range(KE):
                    queries(0, c, ks)
            scores(0, 0)
            scores(0, 1)
            scores(0, 2)
            transposes(0, 0)
            scores(0, 3)
            transposes(0, 1)
            queries(1, 0, range(KD))
            transposes(0, 2)
            queries(1, 1, range(KD))
            transposes(0, 3)
            gate_weights(0)
            gate_weights(1)
            attended(0, 0)
            attended(0, 1)
            scores(1, 0)
            scores(1, 1)
            scores(1, 2)
            transposes(1, 0)
            scores(1, 3)
            transposes(1, 1)
            gate_from_x(0, 0)
            transposes(1, 2)
            from_attended(0, 0)
            gate_from_x(0, 1)
            transposes(1, 3)
            from_attended(0, 1)
            for t in range(2, T):
                gate_from_x(0, t)
                from_attended(0, t)
            attended(1, 0)
            attended(1, 1)
            for t in range(T):
                gate_from_x(1, t)
                from_attended(1, t)


def kernel(x, ctx_1024, L0_xattn_W_mem, L0_xattn_W_gate, L0_xattn_b_gate, L0_xattn_norm_w):
    import numpy as np
    import concourse.bacc as bacc
    from concourse.bass_utils import run_bass_kernel_spmd

    P = 128
    x, mem, wm, wg = (np.asarray(a) for a in (x, ctx_1024, L0_xattn_W_mem, L0_xattn_W_gate))
    B, N, D = x.shape
    M, E = mem.shape[1:]
    KD, KE, KM = D // P, E // P, M // P
    arrays = {
        "xT": x.reshape(B, N, KD, P).transpose(0, 3, 2, 1),
        "ctxT": mem.reshape(B, M, KE, P).transpose(0, 3, 2, 1),
        "ctxN": mem.reshape(B, KM, P, E).transpose(0, 2, 1, 3),
        "w_mem": wm.reshape(KD, P, KE, P).transpose(1, 2, 0, 3),
        "w_memT": wm.reshape(D, KE, P).transpose(2, 1, 0),
        "w_gateT": wg.reshape(D, 2 * KD, P).transpose(2, 1, 0),
        "x_rows": x.reshape(B * N // P, P, D),
        "b_gate": np.asarray(L0_xattn_b_gate),
        "norm_w": np.asarray(L0_xattn_norm_w),
    }
    arrays = {name: np.ascontiguousarray(a) for name, a in arrays.items()}
    nc = bacc.Bacc("TRN2", target_bir_lowering=False, num_devices=1)
    args = [nc.dram_tensor(name, a.shape, mybir.dt.from_np(a.dtype), kind="ExternalInput").ap()
            for name, a in arrays.items()]
    out = nc.dram_tensor("out", (B * N // P, P, D), mybir.dt.float32, kind="ExternalOutput").ap()
    xattn_kernel(nc, *args, out)
    r = run_bass_kernel_spmd(nc, [arrays], core_ids=[0])
    return r.results[0]["out"].reshape(B, N, D)
```

```python
import concourse.bass as bass
from concourse import mybir
from contextlib import ExitStack


def xattn_kernel(nc, xT, ctxT, ctxN, w_mem, w_memT, w_gateT, x_rows, b_gate, norm_w, out):
    f32 = mybir.dt.float32
    f32r = mybir.dt.float32r
    ALU = mybir.AluOpType
    ACT = mybir.ActivationFunctionType
    MAX_OF = bass.bass_isa.ReduceOp.max
    SUM_OF = bass.bass_isa.ReduceOp.add
    Q = 32

    P = 128
    B, _, KD, N = xT.shape
    KE, M = ctxT.shape[2:]
    KM = M // P
    D, E = KD * P, KE * P
    T = N // P
    BANK = 512
    SCALE = float(D) ** -0.5
    EPS = 1e-6
    RING = 7
    WARM = 35
    BANKS = 6
    assert N == BANK and D == BANK and M == 2 * BANK and KE == 2 and T == 4

    ctx = ExitStack()
    with ctx:
        def sb(name, shape, dt=f32):
            return ctx.enter_context(nc.sbuf_tensor(name, shape, dt))

        def pair(name, shape):
            return sb(name + "_hi", shape, f32r), sb(name + "_lo", shape, f32r)

        def sem(name):
            return ctx.enter_context(nc.semaphore(name))

        xT_s = pair("xT", [P, B, KD, N])
        ctxT_s = pair("ctxT", [P, KE, M])
        ctxN_s = pair("ctxN", [P, KM, E])
        wm_s = pair("wm", [P, KE, KD, P])
        wmT_s = pair("wmT", [P, KE, D])
        wgT_s = pair("wgT", [P, 2 * KD, D])
        qT_s = pair("qT", [P, KE, N])
        aT_s = [w[:, KD:KD + KE] for w in wgT_s]
        pT_s = pair("pT", [P, KM, N])
        wcT_s = [w[:].rearrange("p c k n -> p c (k n)") for w in wm_s]

        ring = sb("ring", [P, RING, BANK])
        scores_sb = sb("scores_sb", [P, KM, N])
        top = sb("top", [P, N])
        shift = sb("shift", [P, N])
        warm = sb("warm", [P, P], mybir.dt.bfloat16)
        one = sb("one", [P, 1])
        table = sb("table", [P, 1])
        bias = sb("bias", [P, D])
        gain = sb("gain", [P, D])
        xr = sb("xr", [P, 2, D])
        gx = sb("gx", [P, 2, D])
        gate = sb("gate", [P, 2, D])
        res = sb("res", [P, 2, D])
        inv_sum = sb("inv_sum", [P, B * T])
        half_inv = sb("half_inv", [P, B * T])
        mean_sq = sb("mean_sq", [P, B * T])
        left_sq = sb("left_sq", [P, 2])
        rstd = sb("rstd", [P, B * T])
        neg_half = sb("neg_half", [P, 1])

        wide = ctx.enter_context(nc.psum_tensor("wide", [P, BANKS, BANK], f32))
        acc = ctx.enter_context(nc.psum_tensor("acc", [P, 2, BANK], f32))

        blocks = []
        index_of = {}

        def block(key, src, operand, *place):
            hi, lo = (o[(slice(None), *place)] for o in operand)
            index_of[key] = len(blocks)
            blocks.append((src, hi, lo, key))

        def wm_block(c, half):
            ks = slice(half * KD // 2, (half + 1) * KD // 2)
            block(("wm", c, half), w_mem[:, c, ks], wm_s, c, ks)

        def xT_block(b, k):
            block(("xT", b, k), xT[b, :, k], xT_s, b, k)

        def ctxT_block(b, c, h):
            cols = slice(h * BANK, (h + 1) * BANK)
            block(("ctxT", b, c, h), ctxT[b, :, c, cols], ctxT_s, c, cols)

        def ctxN_block(b, j):
            rows = slice(2 * j, 2 * j + 2)
            block(("ctxN", b, j), ctxN[b, :, rows], ctxN_s, rows)

        def wgT_block(k):
            block(("wgT", k), w_gateT[:, k], wgT_s, k)

        wm_block(0, 0)
        xT_block(0, 0)
        xT_block(0, 1)
        wm_block(1, 0)
        wm_block(0, 1)
        xT_block(0, 2)
        xT_block(0, 3)
        wm_block(1, 1)
        for h in range(2):
            for c in range(KE):
                ctxT_block(0, c, h)
        for k in range(KD):
            xT_block(1, k)
        for k in range(KD, 2 * KD):
            wgT_block(k)
        for j in range(KM // 2):
            ctxN_block(0, j)
        for h in range(2):
            for c in range(KE):
                ctxT_block(1, c, h)
        for k in range(KD):
            wgT_block(k)
        for c in range(KE):
            block(("wmT", c), w_memT[:, c], wmT_s, c)
        for j in range(KM // 2):
            ctxN_block(1, j)
        NB = len(blocks)
        LAST = B * T - 1
        HALVES = (slice(0, D // 2), slice(D // 2, D))

        def slot(i):
            hi = blocks[i][1]
            if len(hi.shape) == 2:
                return ring[:, i % RING, 0:hi.shape[1]]
            a, c = hi.shape[1:]
            return ring[:, i % RING, 0:a * c].rearrange("p (a c) -> p a c", a=a)

        ON_DVE = set(range(0, 12)) | {13, 15, 17} | set(range(20, 28))
        HI_ON_DVE = {20, 21}
        dve_hi = [i for i in range(NB) if i in HI_ON_DVE]
        act_hi = [i for i in range(NB) if i not in HI_ON_DVE]
        dve_lo = [i for i in range(NB) if i in ON_DVE]
        pool_lo = [i for i in range(NB) if i not in ON_DVE]

        loaded = [sem(f"loaded{i}") for i in range(NB)]
        vec_loaded = sem("vec_loaded")
        x_loaded = [sem(f"x_loaded{i}") for i in range(2)]
        stored = [sem(f"stored{i}") for i in range(2)]
        warm_set = sem("warm_set")
        one_set = sem("one_set")
        neg_half_set = sem("neg_half_set")
        act_ready = sem("act_ready")
        hi_act = sem("hi_act")
        hi_dve = sem("hi_dve")
        lo_dve = sem("lo_dve")
        lo_pool = sem("lo_pool")
        q_sum = sem("q_sum")
        scores_sum = sem("scores_sum")
        wc_sum = sem("wc_sum")
        a_sum = sem("a_sum")
        gx_sum = sem("gx_sum")
        ga_sum = sem("ga_sum")
        mc_sum = sem("mc_sum")
        q_hi, q_lo = sem("q_hi"), sem("q_lo")
        copied = sem("copied")
        maxed = sem("maxed")
        shift_set = sem("shift_set")
        shifted = sem("shifted")
        exped = sem("exped")
        pT_hi = sem("pT_hi")
        pT_lo = sem("pT_lo")
        summed = sem("summed")
        total_set = sem("total_set")
        total_turned = sem("total_turned")
        wc_hi, wc_lo = sem("wc_hi"), sem("wc_lo")
        a_hi, a_lo = sem("a_hi"), sem("a_lo")
        inv_done = sem("inv_done")
        half_done = sem("half_done")
        gx_done = sem("gx_done")
        arg_done = sem("arg_done")
        tanh_done = sem("tanh_done")
        gated = sem("gated")
        fused = sem("fused")
        ga_half, mc_half = sem("ga_half"), sem("mc_half")
        gated_half, fused_half = sem("gated_half"), sem("fused_half")
        left_squared, left_ready = sem("left_squared"), sem("left_ready")
        gained, last_gained = sem("gained"), sem("last_gained")
        mean_done = sem("mean_done")
        rstd_done = sem("rstd_done")
        res_done = sem("res_done")
        last_res = sem("last_res")

        def nth_tile(b, t):
            return T * b + t + 1

        def nth_score(b, k):
            return KM * b + k + 1

        def nth_join(b, k):
            return (KM - 1) * b + k

        def nth_chunk(b, c):
            return KE * b + c + 1

        uses = [("scores", 0, k) for k in range(KM)] + [("wc", c) for c in range(KE)]
        uses += [("scores", 1, k) for k in range(KM)]
        for j in range(LAST):
            uses += [("gx", j), ("ga", j), ("mc", j)]
        uses += [("gx", LAST)] + [(use, LAST, h) for use in ("ga", "mc") for h in range(2)]

        def bank(*use):
            return uses.index(use) % BANKS

        def wait_bank(eng, *use):
            n = uses.index(use) - BANKS
            if n < 0:
                return
            kind, i = uses[n][0:2]
            if kind == "scores":
                eng.wait_ge(copied, nth_score(i, uses[n][2]))
            else:
                eng.wait_ge({"wc": wc_lo, "gx": gx_done, "ga": arg_done, "mc": gated}[kind],
                            i + 1)

        def wait_hi(eng, i):
            if i in HI_ON_DVE:
                eng.wait_ge(hi_dve, dve_hi.index(i) + 1)
            else:
                eng.wait_ge(hi_act, act_hi.index(i) + 1)

        def wait_lo(eng, i):
            if i in ON_DVE:
                eng.wait_ge(lo_dve, dve_lo.index(i) + 1)
            else:
                eng.wait_ge(lo_pool, pool_lo.index(i) + 1)

        def wait_place(eng, key):
            if key[0:2] == ("ctxT", 1):
                eng.wait_ge(scores_sum, nth_score(0, KM - 1))
            if key[0:2] == ("ctxN", 1):
                eng.wait_ge(a_sum, nth_chunk(0, KE - 1))

        block_ctx = ctx.enter_context(nc.Block())

        @block_ctx.sync
        def _(sp):
            def load_x(j):
                sp.dma_start(xr[:, j % 2], x_rows[j]).then_inc(x_loaded[j % 2], 16)

            for i, (src, _, _, key) in enumerate(blocks):
                if i >= RING:
                    wait_hi(sp, i - RING)
                    wait_lo(sp, i - RING)
                sp.dma_start(slot(i), src).then_inc(loaded[i], 16)
                if key == ("xT", 1, KD - 1):
                    sp.dma_start(bias[:], b_gate.partition_broadcast(P)).then_inc(vec_loaded, 16)
                    sp.dma_start(gain[:], norm_w.partition_broadcast(P)).then_inc(vec_loaded, 16)
                if key == ("wgT", 0):
                    load_x(0)
                    load_x(1)
            for j in range(LAST):
                sp.wait_ge(res_done, j + 1)
                sp.dma_start(out[j], res[:, j % 2]).then_inc(stored[j % 2], 16)
                if j + 2 < B * T:
                    load_x(j + 2)
            sp.wait_ge(last_res, 1)
            sp.dma_start(out[LAST], res[:, LAST % 2]).then_inc(stored[LAST % 2], 16)
            for done in stored:
                sp.wait_ge(done, 16 * B * T // 2)

        @block_ctx.gpsimd
        def _(pool):
            nc.gpsimd.memset(neg_half[:], -0.5).then_inc(neg_half_set, 1)

            def split_lo(i):
                _, hi, lo, key = blocks[i]
                wait_hi(pool, i)
                wait_place(pool, key)
                nc.gpsimd.tensor_tensor(lo, slot(i), hi.bitcast(f32), ALU.subtract).then_inc(lo_pool, 1)

            def maximum(b):
                pool.wait_ge(maxed, nth_join(b, KM - 1))
                if b:
                    pool.wait_ge(total_turned, b)
                nc.gpsimd.partition_all_reduce(shift[:], top[:], P, MAX_OF).then_inc(shift_set, 1)
                pool.wait_ge(shift_set, b + 1)

            def add_probs(b, k):
                pool.wait_ge(exped, nth_score(b, k))
                if k >= 2:
                    pool.wait_ge(summed, nth_join(b, k - 1))
                nc.gpsimd.tensor_tensor(top[:], scores_sb[:, 0] if k == 1 else top[:], scores_sb[:, k],
                                        ALU.add).then_inc(summed, 1)

            def total(b):
                pool.wait_ge(summed, nth_join(b, KM - 1))
                pool.wait_ge(shifted, nth_score(b, KM - 1))
                nc.gpsimd.partition_all_reduce(shift[:], top[:], P, SUM_OF).then_inc(total_set, 1)

            def gain_rows(j):
                pool.wait_ge(fused, j + 1)
                if j == 0:
                    pool.wait_ge(vec_loaded, 32)
                if j >= 2:
                    pool.wait_ge(stored[j % 2], 16 * (j // 2))
                nc.gpsimd.tensor_tensor(res[:, j % 2], gate[:, j % 2], gain[:], ALU.mult)\
                    .then_inc(gained, 1)

            def norm_factor(j):
                pool.wait_ge(mean_done, j + 1)
                col = slice(j, j + 1)
                nc.gpsimd.tensor_tensor(rstd[:, col], mean_sq[:, col], neg_half[:], ALU.pow)\
                    .then_inc(rstd_done, 1)

            for i in (12, 14, 16, 18, 19):
                split_lo(i)
            maximum(0)
            for k in range(1, KM):
                add_probs(0, k)
            total(0)
            for i in range(28, NB):
                split_lo(i)
            maximum(1)
            pool.wait_ge(neg_half_set, 1)
            add_probs(1, 1)
            for j in range(T - 1):
                gain_rows(j)
                norm_factor(j)
                for k in (2 * j + 2, 2 * j + 3):
                    add_probs(1, k)
            total(1)
            for j in range(T - 1, LAST):
                gain_rows(j)
                norm_factor(j)
            pool.wait_ge(left_squared, 1)
            nc.gpsimd.tensor_scalar(left_sq[:, 1:2], left_sq[:, 0:1], EPS, None, ALU.add)\
                .then_inc(left_ready, 1)
            norm_factor(LAST)

        @block_ctx.scalar
        def _(act):
            act.wait_ge(one_set, 1)
            nc.scalar.activation(table[:], one[:], ACT.Exp).then_inc(act_ready, 1)

            def split_hi(*ids):
                for i in ids:
                    _, hi, _, key = blocks[i]
                    act.wait_ge(loaded[i], 16)
                    wait_place(act, key)
                    nc.scalar.activation(hi, slot(i), ACT.Copy).then_inc(hi_act, 1)

            def query_hi(b, c):
                act.wait_ge(q_sum, nth_chunk(b, c))
                if b:
                    act.wait_ge(scores_sum, nth_score(b - 1, KM - 1))
                nc.scalar.activation(qT_s[0][:, c], acc[:, c], ACT.Copy, scale=SCALE).then_inc(q_hi, 1)

            def copy_scores(b, k):
                act.wait_ge(scores_sum, nth_score(b, k))
                if b:
                    act.wait_ge(pT_lo, nth_score(b - 1, k))
                    act.wait_ge(summed, nth_join(b - 1, max(k, 1)))
                nc.scalar.activation(scores_sb[:, k], wide[:, bank("scores", b, k)], ACT.Copy)\
                    .then_inc(copied, 1)

            def probabilities(b, k):
                act.wait_ge(shifted, nth_score(b, k))
                nc.scalar.activation(scores_sb[:, k], scores_sb[:, k], ACT.Exp).then_inc(exped, 1)
                act.wait_ge(exped, nth_score(b, k))
                if b and k == 0:
                    act.wait_ge(a_sum, nth_chunk(b - 1, KE - 1))
                nc.scalar.activation(pT_s[0][:, k], scores_sb[:, k], ACT.Copy).then_inc(pT_hi, 1)

            def weight_hi(c):
                act.wait_ge(wc_sum, c + 1)
                nc.scalar.activation(wcT_s[0][:, c], wide[:, bank("wc", c)], ACT.Copy).then_inc(wc_hi, 1)

            def attended_hi(b, c):
                act.wait_ge(a_sum, nth_chunk(b, c))
                if b:
                    act.wait_ge(mc_sum, nth_tile(b - 1, T - 1))
                nc.scalar.activation(aT_s[0][:, c], acc[:, c], ACT.Copy).then_inc(a_hi, 1)

            def gate_tanh(j):
                act.wait_ge(arg_done, j + 1)
                nc.scalar.activation(gate[:, j % 2], gate[:, j % 2], ACT.Tanh, scale=0.5)\
                    .then_inc(tanh_done, 1)

            def normalize(j):
                act.wait_ge(gained, j + 1)
                act.wait_ge(rstd_done, j + 1)
                nc.scalar.activation(res[:, j % 2], res[:, j % 2], ACT.Copy,
                                     scale=rstd[:, j:j + 1]).then_inc(res_done, 1)

            split_hi(0, 1, 2, 3, 4, 5, 6, 7, 8, 9)
            query_hi(0, 0)
            split_hi(10)
            query_hi(0, 1)
            split_hi(11, 12, 13)
            for k in range(KM):
                copy_scores(0, k)
                if k < 6:
                    split_hi(14 + k)
            split_hi(22, 23)
            query_hi(1, 0)
            split_hi(24, 25, 26)
            query_hi(1, 1)
            split_hi(27, 28)
            probabilities(0, 0)
            probabilities(0, 1)
            split_hi(29)
            probabilities(0, 2)
            weight_hi(0)
            probabilities(0, 3)
            probabilities(0, 4)
            weight_hi(1)
            probabilities(0, 5)
            split_hi(30)
            probabilities(0, 6)
            probabilities(0, 7)
            split_hi(31, 32, 33)
            attended_hi(0, 0)
            attended_hi(0, 1)
            for k in range(KM):
                copy_scores(1, k)
                if k < 4:
                    split_hi(34 + k)
            gate_tanh(0)
            probabilities(1, 0)
            probabilities(1, 1)
            for j in range(1, T - 1):
                probabilities(1, 2 * j)
                gate_tanh(j)
                normalize(j - 1)
                probabilities(1, 2 * j + 1)
            probabilities(1, KM - 2)
            probabilities(1, KM - 1)
            gate_tanh(T - 1)
            normalize(T - 2)
            attended_hi(1, 0)
            attended_hi(1, 1)
            normalize(T - 1)
            for j in range(T, LAST):
                gate_tanh(j)
                if j < LAST - 1:
                    normalize(j)
            for h, cols in enumerate(HALVES):
                act.wait_ge(arg_done, LAST + h + 1)
                nc.scalar.activation(gate[:, LAST % 2, cols], gate[:, LAST % 2, cols], ACT.Tanh, scale=0.5)\
                    .then_inc(tanh_done, 1)
            normalize(LAST - 1)
            act.wait_ge(fused_half, 1)
            nc.scalar.activation(gx[:, LAST % 2, HALVES[0]], gate[:, LAST % 2, HALVES[0]], ACT.Square,
                                 scale=SCALE, accum_out=left_sq[:, 0:1]).then_inc(left_squared, 1)

        @block_ctx.vector
        def _(dve):
            nc.vector.memset(warm[:].bitcast(mybir.dt.uint32), 0).then_inc(warm_set, 1)
            nc.vector.memset(one[:], 1.0).then_inc(one_set, 1)

            def split(*ids):
                for i in ids:
                    _, hi, _, key = blocks[i]
                    dve.wait_ge(loaded[i], 16)
                    wait_place(dve, key)
                    nc.vector.tensor_copy(hi, slot(i)).then_inc(hi_dve, 1)
                split_lo(*ids)

            def split_lo(*ids):
                for i in ids:
                    _, hi, lo, key = blocks[i]
                    wait_hi(dve, i)
                    wait_place(dve, key)
                    nc.vector.tensor_tensor(lo, slot(i), hi.bitcast(f32), ALU.subtract).then_inc(lo_dve, 1)

            def query_lo(b, c):
                dve.wait_ge(q_hi, nth_chunk(b, c))
                nc.vector.scalar_tensor_tensor(out=qT_s[1][:, c], in0=acc[:, c], scalar=SCALE,
                                               in1=qT_s[0][:, c].bitcast(f32), op0=ALU.mult,
                                               op1=ALU.subtract).then_inc(q_lo, 1)

            def running_max(b, k):
                dve.wait_ge(copied, nth_score(b, k))
                if k == 1:
                    if b:
                        dve.wait_ge(inv_done, b * P // Q)
                else:
                    dve.wait_ge(maxed, nth_join(b, k - 1))
                nc.vector.tensor_tensor(top[:], scores_sb[:, k],
                                        scores_sb[:, 0] if k == 1 else top[:], ALU.max).then_inc(maxed, 1)

            def shift_scores(b, k):
                dve.wait_ge(shift_set, b + 1)
                dve.wait_ge(copied, nth_score(b, k))
                nc.vector.tensor_tensor(scores_sb[:, k], scores_sb[:, k], shift[:], ALU.subtract)\
                    .then_inc(shifted, 1)

            def probs_lo(b, k):
                dve.wait_ge(pT_hi, nth_score(b, k))
                nc.vector.tensor_tensor(pT_s[1][:, k], scores_sb[:, k], pT_s[0][:, k].bitcast(f32),
                                        ALU.subtract).then_inc(pT_lo, 1)

            def weight_lo(c):
                dve.wait_ge(wc_hi, c + 1)
                nc.vector.tensor_tensor(wcT_s[1][:, c], wide[:, bank("wc", c)], wcT_s[0][:, c].bitcast(f32),
                                        ALU.subtract).then_inc(wc_lo, 1)

            def attended_lo(b, c):
                dve.wait_ge(a_hi, nth_chunk(b, c))
                nc.vector.tensor_tensor(aT_s[1][:, c], acc[:, c], aT_s[0][:, c].bitcast(f32),
                                        ALU.subtract).then_inc(a_lo, 1)

            def inverses(b):
                cols = slice(T * b, T * b + T)
                dve.wait_ge(total_set, b + 1)
                nc.vector.transpose(top[:], shift[:]).then_inc(total_turned, 1)
                dve.wait_ge(total_turned, b + 1)
                by_tile = top[:].rearrange("p (t n) -> p t n", t=T)
                for q in range(P // Q):
                    rows = slice(q * Q, (q + 1) * Q)
                    nc.vector.reciprocal(inv_sum[rows, cols], by_tile[rows, :, q * Q]).then_inc(inv_done, 1)
                dve.wait_ge(inv_done, (b + 1) * P // Q)
                nc.vector.tensor_scalar(half_inv[:, cols], inv_sum[:, cols], 0.5, None, ALU.mult)\
                    .then_inc(half_done, 1)

            def gate_x(b, t):
                j = T * b + t
                if j == 0:
                    dve.wait_ge(vec_loaded, 32)
                if j >= 2:
                    dve.wait_ge(mean_done, j - 1)
                dve.wait_ge(gx_sum, j + 1)
                nc.vector.tensor_tensor(gx[:, j % 2], wide[:, bank("gx", j)], bias[:], ALU.add)\
                    .then_inc(gx_done, 1)

            def gate_arg(b, t):
                j = T * b + t
                dve.wait_ge(gx_done, j + 1)
                dve.wait_ge(ga_sum, j + 1)
                if j >= 2:
                    dve.wait_ge(gained, j - 1)
                nc.vector.scalar_tensor_tensor(out=gate[:, j % 2], in0=wide[:, bank("ga", j)],
                                               scalar=inv_sum[:, j:j + 1], in1=gx[:, j % 2],
                                               op0=ALU.mult, op1=ALU.add).then_inc(arg_done, 1)

            def gated_context(b, t):
                j = T * b + t
                dve.wait_ge(tanh_done, j + 1)
                dve.wait_ge(mc_sum, j + 1)
                nc.vector.scalar_tensor_tensor(out=gate[:, j % 2], in0=gate[:, j % 2], scalar=1.0,
                                               in1=wide[:, bank("mc", j)], op0=ALU.add,
                                               op1=ALU.mult).then_inc(gated, 1)

            def fuse(b, t):
                j = T * b + t
                dve.wait_ge(gated, j + 1)
                dve.wait_ge(half_done, b + 1)
                dve.wait_ge(x_loaded[j % 2], 16 * (j // 2 + 1))
                nc.vector.scalar_tensor_tensor(out=gate[:, j % 2], in0=gate[:, j % 2],
                                               scalar=half_inv[:, j:j + 1], in1=xr[:, j % 2],
                                               op0=ALU.mult, op1=ALU.add).then_inc(fused, 1)

            def mean_square(j):
                dve.wait_ge(fused, j + 1)
                nc.vector.tensor_tensor_reduce(gx[:, j % 2], gate[:, j % 2], gate[:, j % 2], 1.0 / D, EPS,
                                               ALU.mult, ALU.add, mean_sq[:, j:j + 1]).then_inc(mean_done, 1)

            def finish(b, t):
                gated_context(b, t)
                fuse(b, t)
                mean_square(T * b + t)

            def finish_last():
                n = LAST % 2
                dve.wait_ge(gx_done, LAST + 1)
                dve.wait_ge(gained, LAST - 1)
                for h, cols in enumerate(HALVES):
                    dve.wait_ge(ga_half, h + 1)
                    nc.vector.scalar_tensor_tensor(out=gate[:, n, cols],
                                                   in0=wide[:, bank("ga", LAST, h), cols],
                                                   scalar=inv_sum[:, LAST:], in1=gx[:, n, cols],
                                                   op0=ALU.mult, op1=ALU.add).then_inc(arg_done, 1)
                dve.wait_ge(x_loaded[n], 16 * (LAST // 2 + 1))

                def gated_half_row(h, cols):
                    dve.wait_ge(tanh_done, LAST + h + 1)
                    dve.wait_ge(mc_half, h + 1)
                    nc.vector.scalar_tensor_tensor(out=gate[:, n, cols], in0=gate[:, n, cols],
                                                   scalar=1.0, in1=wide[:, bank("mc", LAST, h), cols],
                                                   op0=ALU.add, op1=ALU.mult).then_inc(gated_half, 1)

                def fused_half_row(h, cols):
                    dve.wait_ge(gated_half, h + 1)
                    nc.vector.scalar_tensor_tensor(out=gate[:, n, cols], in0=gate[:, n, cols],
                                                   scalar=half_inv[:, LAST:], in1=xr[:, n, cols],
                                                   op0=ALU.mult, op1=ALU.add).then_inc(fused_half, 1)

                for h, cols in enumerate(HALVES):
                    gated_half_row(h, cols)
                    fused_half_row(h, cols)
                dve.wait_ge(fused_half, 2)
                dve.wait_ge(left_ready, 1)
                nc.vector.tensor_tensor_reduce(gx[:, n, cols], gate[:, n, cols], gate[:, n, cols],
                                               1.0 / D, left_sq[:, 1:2], ALU.mult, ALU.add,
                                               mean_sq[:, LAST:]).then_inc(mean_done, 1)
                dve.wait_ge(stored[n], 16 * (LAST // 2))
                nc.vector.tensor_tensor(res[:, n], gate[:, n], gain[:], ALU.mult).then_inc(last_gained, 1)
                dve.wait_ge(last_gained, 1)
                dve.wait_ge(rstd_done, LAST + 1)
                nc.vector.tensor_scalar(res[:, n], res[:, n], rstd[:, LAST:], None, ALU.mult)\
                    .then_inc(last_res, 1)

            split_lo(0, 1, 2, 3, 4, 5, 6, 7, 8, 9)
            query_lo(0, 0)
            split_lo(10)
            query_lo(0, 1)
            split_lo(11, 13)
            running_max(0, 1)
            running_max(0, 2)
            split_lo(15)
            running_max(0, 3)
            split_lo(17)
            running_max(0, 4)
            split(20)
            running_max(0, 5)
            split(21)
            running_max(0, 6)
            running_max(0, 7)
            split_lo(22, 23)
            query_lo(1, 0)
            split_lo(24, 25)
            query_lo(1, 1)
            shift_scores(0, 0)
            shift_scores(0, 1)
            shift_scores(0, 2)
            split_lo(26)
            probs_lo(0, 0)
            shift_scores(0, 3)
            probs_lo(0, 1)
            shift_scores(0, 4)
            weight_lo(0)
            probs_lo(0, 2)
            shift_scores(0, 5)
            probs_lo(0, 3)
            shift_scores(0, 6)
            probs_lo(0, 4)
            weight_lo(1)
            shift_scores(0, 7)
            probs_lo(0, 5)
            probs_lo(0, 6)
            probs_lo(0, 7)
            split_lo(27)
            attended_lo(0, 0)
            attended_lo(0, 1)
            inverses(0)
            for k in range(1, KM):
                running_max(1, k)
            gate_x(0, 0)
            gate_arg(0, 0)
            shift_scores(1, 0)
            shift_scores(1, 1)
            finish(0, 0)
            for t in range(1, T - 1):
                probs_lo(1, 2 * t - 2)
                gate_x(0, t)
                shift_scores(1, 2 * t)
                gate_arg(0, t)
                probs_lo(1, 2 * t - 1)
                shift_scores(1, 2 * t + 1)
                finish(0, t)
            probs_lo(1, KM - 4)
            shift_scores(1, KM - 2)
            gate_x(0, T - 1)
            shift_scores(1, KM - 1)
            gate_arg(0, T - 1)
            probs_lo(1, KM - 3)
            probs_lo(1, KM - 2)
            probs_lo(1, KM - 1)
            finish(0, T - 1)
            attended_lo(1, 0)
            attended_lo(1, 1)
            inverses(1)
            for t in range(T - 1):
                gate_x(1, t)
                gate_arg(1, t)
                finish(1, t)
            gate_x(1, T - 1)
            finish_last()

        @block_ctx.tensor
        def _(pe):
            HI, LO = 0, 1
            PASSES = ((HI, HI), (HI, LO), (LO, HI))

            def keep_warm(n):
                for _ in range(n):
                    nc.tensor.matmul(wide[:, BANKS - 1, 0:P], warm[:], warm[:], start=True, stop=True)

            def product(psum, terms, done):
                n = 0
                for left, right in PASSES:
                    for stationary, moving, wait in terms:
                        if (left, right) == (HI, HI) and wait is not None:
                            wait(HI)
                        if (left, right) == (HI, LO) and wait is not None:
                            wait(LO)
                        last = nc.tensor.matmul(psum, stationary(left), moving(right), start=(n == 0),
                                                stop=(n == 3 * len(terms) - 1))
                        n += 1
                last.then_inc(done, 1)

            def input_wait(key):
                def wait(half):
                    if half == HI:
                        wait_hi(pe, index_of[key])
                    else:
                        wait_lo(pe, index_of[key])
                return wait

            def queries(b, c, ks):
                if b and ks[0] == 0:
                    pe.wait_ge(q_lo, nth_chunk(b - 1, c))
                for k in ks:
                    wm_i, xT_i = index_of["wm", c, 2 * k // KD], index_of["xT", b, k]
                    for left, right in ((HI, HI), (LO, HI), (HI, LO)):
                        if (left, right) == (HI, HI):
                            wait_hi(pe, wm_i)
                            wait_hi(pe, xT_i)
                        elif left == LO:
                            wait_lo(pe, wm_i)
                        else:
                            wait_lo(pe, xT_i)
                        last = nc.tensor.matmul(acc[:, c], wm_s[left][:, c, k], xT_s[right][:, b, k],
                                                start=(k == 0 and (left, right) == (HI, HI)),
                                                stop=(k == KD - 1 and (left, right) == (HI, LO)))
                if ks[-1] == KD - 1:
                    last.then_inc(q_sum, 1)

            def scores(b, *ks):
                for c in range(KE):
                    for k in ks:
                        if c == 0:
                            wait_bank(pe, "scores", b, k)
                        i = index_of["ctxT", b, c, k * P // BANK]
                        first = k * P % BANK == 0
                        for left, right in ((HI, HI), (LO, HI), (HI, LO)):
                            if (left, right) == (HI, HI) and first:
                                wait_hi(pe, i)
                                pe.wait_ge(q_hi, nth_chunk(b, c))
                            if left == LO and first:
                                wait_lo(pe, i)
                            if right == LO and first:
                                pe.wait_ge(q_lo, nth_chunk(b, c))
                            last = nc.tensor.matmul(wide[:, bank("scores", b, k)],
                                                    ctxT_s[left][:, c, k * P:(k + 1) * P],
                                                    qT_s[right][:, c],
                                                    start=(c == 0 and (left, right) == (HI, HI)),
                                                    stop=(c == KE - 1 and right == LO))
                        if c == KE - 1:
                            last.then_inc(scores_sum, 1)

            def gate_weights(c):
                wait_bank(pe, "wc", c)
                product(wide[:, bank("wc", c)],
                        [(lambda s, k=k: wm_s[s][:, c, k], lambda s, k=k: wgT_s[s][:, KD + k],
                          input_wait(("wgT", KD + k))) for k in range(KD)], wc_sum)

            def attended(b):
                if b == 0:
                    pe.wait_ge(q_lo, nth_chunk(1, KE - 1))
                else:
                    pe.wait_ge(a_lo, nth_chunk(b - 1, KE - 1))
                for k in range(KM):
                    ctx_i = index_of["ctxN", b, k // 2]
                    for left, right in ((HI, HI), (LO, HI), (HI, LO)):
                        if (left, right) == (HI, HI):
                            wait_hi(pe, ctx_i)
                            pe.wait_ge(pT_hi, nth_score(b, k))
                        elif left == LO:
                            wait_lo(pe, ctx_i)
                        else:
                            pe.wait_ge(pT_lo, nth_score(b, k))
                        for c in range(KE):
                            last = nc.tensor.matmul(acc[:, c], ctxN_s[left][:, k, c * P:(c + 1) * P],
                                                    pT_s[right][:, k],
                                                    start=(k == 0 and (left, right) == (HI, HI)),
                                                    stop=(k == KM - 1 and right == LO))
                            if k == KM - 1 and right == LO:
                                last.then_inc(a_sum, 1)

            def gate_from_x(b, t):
                j = T * b + t
                wait_bank(pe, "gx", j)
                rows = slice(t * P, (t + 1) * P)
                product(wide[:, bank("gx", j)],
                        [(lambda s, k=k: xT_s[s][:, b, k, rows], lambda s, k=k: wgT_s[s][:, k],
                          input_wait(("wgT", k)) if j == 0 else None) for k in range(KD)], gx_sum)

            def from_attended(b, t):
                j = T * b + t
                rows = slice(t * P, (t + 1) * P)
                if t == 0:
                    pe.wait_ge(a_lo, nth_chunk(b, KE - 1))
                if j == 0:
                    pe.wait_ge(wc_lo, KE)
                whole = slice(0, D)
                for use, weights, done, done_half in (("ga", wcT_s, ga_sum, ga_half),
                                                      ("mc", wmT_s, mc_sum, mc_half)):
                    for h, cols in enumerate(HALVES if j == LAST else (whole,)):
                        key = (use, j, h) if j == LAST else (use, j)
                        wait_bank(pe, *key)
                        product(wide[:, bank(*key), cols],
                                [(lambda s, c=c: aT_s[s][:, c, rows], lambda s, c=c: weights[s][:, c, cols],
                                  input_wait(("wmT", c)) if j == 0 and use == "mc" else None)
                                 for c in range(KE)], done_half if j == LAST else done)

            pe.wait_ge(warm_set, 1)
            keep_warm(WARM)
            halves = (range(0, KD // 2), range(KD // 2, KD))
            for ks in halves:
                for c in range(KE):
                    queries(0, c, ks)
            scores(0, 0, 1, 2)
            for k in range(3, KM):
                scores(0, k)
            queries(1, 0, range(KD))
            queries(1, 1, range(KD))
            gate_weights(0)
            gate_weights(1)
            attended(0)
            for k in range(KM):
                scores(1, k)
            for t in range(T):
                gate_from_x(0, t)
                from_attended(0, t)
            attended(1)
            for t in range(T):
                gate_from_x(1, t)
                from_attended(1, t)


def kernel(x, ctx_1024, L0_xattn_W_mem, L0_xattn_W_gate, L0_xattn_b_gate, L0_xattn_norm_w):
    import numpy as np
    import concourse.bacc as bacc
    from concourse.bass_utils import run_bass_kernel_spmd

    P = 128
    x, mem, wm, wg = (np.asarray(a) for a in (x, ctx_1024, L0_xattn_W_mem, L0_xattn_W_gate))
    B, N, D = x.shape
    M, E = mem.shape[1:]
    KD, KE, KM = D // P, E // P, M // P
    arrays = {
        "xT": x.reshape(B, N, KD, P).transpose(0, 3, 2, 1),
        "ctxT": mem.reshape(B, M, KE, P).transpose(0, 3, 2, 1),
        "ctxN": mem.reshape(B, KM, P, E).transpose(0, 2, 1, 3),
        "w_mem": wm.reshape(KD, P, KE, P).transpose(1, 2, 0, 3),
        "w_memT": wm.reshape(D, KE, P).transpose(2, 1, 0),
        "w_gateT": wg.reshape(D, 2 * KD, P).transpose(2, 1, 0),
        "x_rows": x.reshape(B * N // P, P, D),
        "b_gate": np.asarray(L0_xattn_b_gate),
        "norm_w": np.asarray(L0_xattn_norm_w),
    }
    arrays = {name: np.ascontiguousarray(a) for name, a in arrays.items()}
    nc = bacc.Bacc("TRN2", target_bir_lowering=False, num_devices=1)
    args = [nc.dram_tensor(name, a.shape, mybir.dt.from_np(a.dtype), kind="ExternalInput").ap()
            for name, a in arrays.items()]
    out = nc.dram_tensor("out", (B * N // P, P, D), mybir.dt.float32, kind="ExternalOutput").ap()
    xattn_kernel(nc, *args, out)
    r = run_bass_kernel_spmd(nc, [arrays], core_ids=[0])
    return r.results[0]["out"].reshape(B, N, D)
```
